# Optimizing a Trainium2 kernel written in Bass

```python
import numpy as np
import jax
import jax.numpy as jnp

def _softmax(x, axis=-1):
    return jax.nn.softmax(x, axis=axis)

def _gelu(x):
    return jax.nn.gelu(x, approximate=True)

def _silu(x):
    return jax.nn.silu(x)

def _sigmoid(x):
    return jax.nn.sigmoid(x)

def _layernorm(x, axis=-1, eps=1e-05):
    m = jnp.mean(x, axis=axis, keepdims=True)
    v = jnp.var(x, axis=axis, keepdims=True)
    return (x - m) / jnp.sqrt(v + eps)

def _scatter_add(tgt, idx, src, axis=0):
    return tgt.at[idx].add(src)

def _segment_sum(src, seg, n):
    return jax.ops.segment_sum(src, seg, n)
kernel_name = 'mk_xattn_ffn_d1_seqx_r8_006601'

def setup_inputs(seed: int=0):
    np.random.seed(seed)
    _w = jnp.asarray

    def _rec_inputs():
        import jax
        import jax.numpy as jnp
        _rk = jax.random.key(seed)
        x = 7.22e-05 + 1 * jax.random.normal(jax.random.fold_in(_rk, 1), (16, 128, 256), jnp.float32)
        _lenS = 128 - jax.random.randint(jax.random.fold_in(_rk, 7), (16,), 0, max(1, 128 // 4) + 1, jnp.int32)
        _lenS2 = 128 - jax.random.randint(jax.random.fold_in(_rk, 8), (16,), 0, max(1, 128 // 4) + 1, jnp.int32)
        _ctx_1024P = jax.random.normal(jax.random.fold_in(_rk, 11), (16, 16, 128), jnp.float32)
        _ctx_1024c = jax.random.dirichlet(jax.random.fold_in(_rk, 511), 0.3 * jnp.ones((16,), jnp.float32), (16, 128))
        _ctx_1024t = jnp.einsum('bsk,bkd->bsd', _ctx_1024c, _ctx_1024P)
        _ctx_1024t = _ctx_1024t * jax.lax.rsqrt(jnp.mean(jnp.square(_ctx_1024t)) + 1e-12) * 0.953939
        ctx_1024 = -1.39393e-06 + 0.999914 * (_ctx_1024t + 0.3 * jax.random.normal(jax.random.fold_in(_rk, 611), (16, 128, 128), jnp.float32))
        fside_BxSx2_0 = jax.random.uniform(jax.random.fold_in(_rk, 12), (16, 128, 2), jnp.float32, 0.0, 0.999707)
        return (x, ctx_1024, fside_BxSx2_0)
    x, ctx_1024, fside_BxSx2_0 = _rec_inputs()

    def _L0_xattn_setup():
        import jax, jax.numpy as jnp
        import numpy as np
        DIM = 256
        CTX_DIM = 128
        N_HEADS = 32
        HEAD_DIM = DIM // N_HEADS
        POS_DIM = 2
        B, N, CTXN = (2, 256, 256)
        ROPE_BASE = 10000.0

        def apply_axial_rope(x, pos):
            b, n, h, d = x.shape
            p = pos.shape[-1]
            dpa = d // p
            half = dpa // 2
            freqs = ROPE_BASE ** (-jnp.arange(half, dtype=x.dtype) / half)
            ang = pos[..., :, None] * freqs
            cos = jnp.cos(ang)[:, :, None, :, :]
            sin = jnp.sin(ang)[:, :, None, :, :]
            xr = x.reshape(b, n, h, p, half, 2)
            x1, x2 = (xr[..., 0], xr[..., 1])
            out = jnp.stack([x1 * cos - x2 * sin, x1 * sin + x2 * cos], axis=-1)
            return out.reshape(b, n, h, d)
        key = jax.random.key(seed)
        ks = jax.random.split(key, 8)
        x = jax.random.normal(ks[0], (B, N, DIM), jnp.float32)
        ctx = jax.random.normal(ks[1], (B, CTXN, CTX_DIM), jnp.float32)
        pos_map = jax.random.uniform(ks[2], (B, N, POS_DIM), jnp.float32)
        ctx_pos_map = jax.random.uniform(ks[3], (B, CTXN, POS_DIM), jnp.float32)
        Wq = jax.random.normal(ks[4], (DIM, DIM), jnp.float32) / np.sqrt(DIM)
        Wkv = jax.random.normal(ks[5], (CTX_DIM, 2 * DIM), jnp.float32) / np.sqrt(CTX_DIM)
        Wout = jax.random.normal(ks[6], (DIM, DIM), jnp.float32) / np.sqrt(DIM)
        bout = jnp.zeros((DIM,), jnp.float32)
        return {'x': x, 'ctx': ctx, 'pos_map': pos_map, 'ctx_pos_map': ctx_pos_map, 'Wq': Wq, 'Wkv': Wkv, 'Wout': Wout, 'bout': bout}
    _L0_xattn_all = _L0_xattn_setup()
    _L0_xattn_in = {k: v for k, v in _L0_xattn_all.items() if k in ('Wq', 'Wkv', 'Wout', 'bout')}
    del _L0_xattn_all

    def _L0_ffn_setup():
        import jax, jax.numpy as jnp
        import numpy as np
        B, S, H = (1, 128, 256)
        I = 176
        E = 32
        K = 6
        G = 8
        TG = 3
        NSH = 2
        SCALE = 16.0
        C = 48

        def _moe_forward(x3, gate_w, w_gate_up, w_down, ws_gate_up, ws_down):
            b, s, h = x3.shape
            x = x3.reshape(-1, h)
            T = x.shape[0]
            logits = x @ gate_w.T
            grouped = logits.reshape(T, G, E // G)
            group_scores = jnp.max(grouped, axis=-1)
            _, group_idx = jax.lax.top_k(group_scores, TG)
            group_keep = jnp.zeros((T, G), bool).at[jnp.arange(T)[:, None], group_idx].set(True)
            masked = jnp.where(group_keep[..., None], grouped, 0.0)
            scores = masked.reshape(T, E)
            probs = jax.nn.softmax(scores.astype(jnp.float32), axis=-1)
            topk_w, topk_idx = jax.lax.top_k(probs, K)
            topk_w = topk_w * SCALE
            flat_e = topk_idx.reshape(-1)
            tok_idx = jnp.repeat(jnp.arange(T), K)
            oh = jax.nn.one_hot(flat_e, E, dtype=jnp.int32)
            pos = jnp.take_along_axis(jnp.cumsum(oh, axis=0) - 1, flat_e[:, None], axis=1)[:, 0]
            valid = pos < C
            slot = jnp.where(valid, flat_e * C + pos, E * C)
            buf = jnp.zeros((E * C + 1, h), x.dtype).at[slot].set(x[tok_idx])
            xb = buf[:E * C].reshape(E, C, h)
            gu = jnp.einsum('ech,ehf->ecf', xb, w_gate_up)
            g, u = jnp.split(gu, 2, axis=-1)
            act = jax.nn.silu(g) * u
            yb = jnp.einsum('eci,eih->ech', act, w_down)
            yflat = jnp.concatenate([yb.reshape(E * C, h), jnp.zeros((1, h), yb.dtype)], axis=0)
            y_pairs = yflat[slot].reshape(T, K, h)
            out = jnp.einsum('tk,tkh->th', topk_w.astype(x.dtype), y_pairs)
            gu_s = x @ ws_gate_up
            gs, us = jnp.split(gu_s, 2, axis=-1)
            out = out + jax.nn.silu(gs) * us @ ws_down
            return out.reshape(b, s, h)
        key = jax.random.key(seed)
        ks = jax.random.split(key, 6)
        s = 0.02
        return {'hidden_states': jax.random.normal(ks[0], (B, S, H), jnp.float32), 'gate_w': jax.random.normal(ks[1], (E, H), jnp.float32) * s, 'w_gate_up': jax.random.normal(ks[2], (E, H, 2 * I), jnp.float32) * s, 'w_down': jax.random.normal(ks[3], (E, I, H), jnp.float32) * s, 'ws_gate_up': jax.random.normal(ks[4], (H, 2 * I * NSH), jnp.float32) * s, 'ws_down': jax.random.normal(ks[5], (I * NSH, H), jnp.float32) * s}
    _L0_ffn_all = _L0_ffn_setup()
    _L0_ffn_in = {k: v for k, v in _L0_ffn_all.items() if k in ('gate_w', 'w_gate_up', 'w_down', 'ws_gate_up', 'ws_down')}
    del _L0_ffn_all
    return {'x': x, 'ctx_1024': ctx_1024, 'fside_BxSx2_0': fside_BxSx2_0, 'L0_xattn_Wq': _L0_xattn_in['Wq'], 'L0_xattn_Wkv': _L0_xattn_in['Wkv'], 'L0_xattn_Wout': _L0_xattn_in['Wout'], 'L0_xattn_bout': _L0_xattn_in['bout'], 'L0_ffn_gate_w': _L0_ffn_in['gate_w'], 'L0_ffn_w_gate_up': _L0_ffn_in['w_gate_up'], 'L0_ffn_w_down': _L0_ffn_in['w_down'], 'L0_ffn_ws_gate_up': _L0_ffn_in['ws_gate_up'], 'L0_ffn_ws_down': _L0_ffn_in['ws_down']}

def reference(x, ctx_1024, fside_BxSx2_0, L0_xattn_Wq, L0_xattn_Wkv, L0_xattn_Wout, L0_xattn_bout, L0_ffn_gate_w, L0_ffn_w_gate_up, L0_ffn_w_down, L0_ffn_ws_gate_up, L0_ffn_ws_down):
    import jax
    import jax.numpy as jnp

    def _L0_xattn_ref(x, ctx, pos_map, ctx_pos_map, Wq, Wkv, Wout, bout):
        import jax, jax.numpy as jnp
        import numpy as np
        DIM = 256
        CTX_DIM = 128
        N_HEADS = 32
        HEAD_DIM = DIM // N_HEADS
        POS_DIM = 2
        B, N, CTXN = (2, 256, 256)
        ROPE_BASE = 10000.0

        def apply_axial_rope(x, pos):
            b, n, h, d = x.shape
            p = pos.shape[-1]
            dpa = d // p
            half = dpa // 2
            freqs = ROPE_BASE ** (-jnp.arange(half, dtype=x.dtype) / half)
            ang = pos[..., :, None] * freqs
            cos = jnp.cos(ang)[:, :, None, :, :]
            sin = jnp.sin(ang)[:, :, None, :, :]
            xr = x.reshape(b, n, h, p, half, 2)
            x1, x2 = (xr[..., 0], xr[..., 1])
            out = jnp.stack([x1 * cos - x2 * sin, x1 * sin + x2 * cos], axis=-1)
            return out.reshape(b, n, h, d)
        b, n, _ = x.shape
        ctx_n = ctx.shape[1]
        q = (x @ Wq).reshape(b, n, N_HEADS, HEAD_DIM)
        k, v = jnp.split(ctx @ Wkv, 2, axis=-1)
        k = k.reshape(b, ctx_n, N_HEADS, HEAD_DIM)
        v = v.reshape(b, ctx_n, N_HEADS, HEAD_DIM)
        q = apply_axial_rope(q, pos_map)
        k = apply_axial_rope(k, ctx_pos_map)
        scale = 1.0 / np.sqrt(HEAD_DIM).astype(np.float32)
        logits = jnp.einsum('bqhd,bkhd->bhqk', q, k) * scale
        w = jax.nn.softmax(logits, axis=-1)
        attn = jnp.einsum('bhqk,bkhd->bqhd', w, v)
        attn = attn.reshape(b, n, N_HEADS * HEAD_DIM)
        return attn @ Wout + bout

    def _L0_ffn_ref(hidden_states, gate_w, w_gate_up, w_down, ws_gate_up, ws_down):
        import jax, jax.numpy as jnp
        import numpy as np
        B, S, H = (1, 128, 256)
        I = 176
        E = 32
        K = 6
        G = 8
        TG = 3
        NSH = 2
        SCALE = 16.0
        C = 48

        def _moe_forward(x3, gate_w, w_gate_up, w_down, ws_gate_up, ws_down):
            b, s, h = x3.shape
            x = x3.reshape(-1, h)
            T = x.shape[0]
            logits = x @ gate_w.T
            grouped = logits.reshape(T, G, E // G)
            group_scores = jnp.max(grouped, axis=-1)
            _, group_idx = jax.lax.top_k(group_scores, TG)
            group_keep = jnp.zeros((T, G), bool).at[jnp.arange(T)[:, None], group_idx].set(True)
            masked = jnp.where(group_keep[..., None], grouped, 0.0)
            scores = masked.reshape(T, E)
            probs = jax.nn.softmax(scores.astype(jnp.float32), axis=-1)
            topk_w, topk_idx = jax.lax.top_k(probs, K)
            topk_w = topk_w * SCALE
            flat_e = topk_idx.reshape(-1)
            tok_idx = jnp.repeat(jnp.arange(T), K)
            oh = jax.nn.one_hot(flat_e, E, dtype=jnp.int32)
            pos = jnp.take_along_axis(jnp.cumsum(oh, axis=0) - 1, flat_e[:, None], axis=1)[:, 0]
            valid = pos < C
            slot = jnp.where(valid, flat_e * C + pos, E * C)
            buf = jnp.zeros((E * C + 1, h), x.dtype).at[slot].set(x[tok_idx])
            xb = buf[:E * C].reshape(E, C, h)
            gu = jnp.einsum('ech,ehf->ecf', xb, w_gate_up)
            g, u = jnp.split(gu, 2, axis=-1)
            act = jax.nn.silu(g) * u
            yb = jnp.einsum('eci,eih->ech', act, w_down)
            yflat = jnp.concatenate([yb.reshape(E * C, h), jnp.zeros((1, h), yb.dtype)], axis=0)
            y_pairs = yflat[slot].reshape(T, K, h)
            out = jnp.einsum('tk,tkh->th', topk_w.astype(x.dtype), y_pairs)
            gu_s = x @ ws_gate_up
            gs, us = jnp.split(gu_s, 2, axis=-1)
            out = out + jax.nn.silu(gs) * us @ ws_down
            return out.reshape(b, s, h)
        return _moe_forward(hidden_states, gate_w, w_gate_up, w_down, ws_gate_up, ws_down)
    x = x + _L0_xattn_ref(_layernorm(x, axis=-1), ctx_1024, fside_BxSx2_0, fside_BxSx2_0, L0_xattn_Wq, L0_xattn_Wkv, L0_xattn_Wout, L0_xattn_bout)
    x = x + _L0_ffn_ref(_layernorm(x, axis=-1), L0_ffn_gate_w, L0_ffn_w_gate_up, L0_ffn_w_down, L0_ffn_ws_gate_up, L0_ffn_ws_down)
    return x

_drawn_inputs = setup_inputs


def setup_inputs(seed=0):
    import zlib

    import numpy as np

    out = dict(_drawn_inputs(seed))
    spreads = {'L0_xattn_bout': (0.0, 0.1)}
    factors = {'L0_ffn_gate_w': 3.912,
     'L0_ffn_w_gate_up': 2.972,
     'L0_ffn_w_down': 2.91,
     'L0_ffn_ws_gate_up': 3.235,
     'L0_ffn_ws_down': 3.263}
    for name, (base, spread) in spreads.items():
        noise = np.random.default_rng([zlib.crc32(name.encode()), seed]).standard_normal(out[name].shape)
        drawn = base * np.exp(spread * noise) if base else spread * noise
        out[name] = jnp.asarray(drawn.astype(out[name].dtype))
    for name, factor in factors.items():
        out[name] = (out[name] * factor).astype(out[name].dtype)
    return out
```

```python
from contextlib import ExitStack

import numpy as np

import concourse.bass as bass
from concourse import mybir

ALU = mybir.AluOpType
ACT = mybir.ActivationFunctionType
AX = mybir.AxisListType
F32 = mybir.dt.float32
F16 = mybir.dt.float16
U32 = mybir.dt.uint32

P = 128
NB, D, DC = 16, 256, 128
NH, HD = 32, 8
QUADS, SLOT = NH // 4, 32
DK = D // P
MAXROW = 3 * HD
SCALE = float(1.0 / np.sqrt(np.float32(HD)))
EPS = 1e-5
TWO_PI = 6.283185
BIG = 12582912.0
NE, INNER, TOPK, CAP = 32, 176, 6, 48
GROUPS, TOPG = 8, 3
SHARED = 2 * INNER
ROUTE_SCALE = 16.0
HALF, LOT = NE // 2, 4
IH = INNER // 2
T = NB * P
COUNT_ACT = 4


class Batch:

    def __init__(self, half, par):
        self.half, self.par = half + par // 2, par % 2
        self.n = 2 * self.half + self.par

    def __add__(self, k):
        return Batch(self.half, self.par + k) if k >= 0 or self.par + k >= 0 else Batch(self.half - 1, self.par + k + 2)


def at_least(eng, sem, count):
    if not isinstance(count, int) or count > 0:
        eng.wait_ge(sem, count)


def build(nc, x, ctx_in, pos, wq, wkv, wout, bout, gate_w, w_gu, w_dn, ws_gu, ws_dn, out):
    with ExitStack() as es:
        def keep(name, shape, dt=F32):
            return es.enter_context(nc.sbuf_tensor(name, shape, dt))

        def sem(name):
            return es.enter_context(nc.semaphore(name))

        X = keep("X", [P, NB, D])
        identf = keep("identf", [P, P])
        st2 = keep("st2", [P, NB, 6])
        ring = Ring(nc, keep, sem, w_gu, w_dn)
        attention(nc, sem, X, identf, st2, ring, x, ctx_in, pos, wq, wkv, wout, bout)
        mixture(nc, sem, X, identf, st2, ring, gate_w, ws_gu, ws_dn, out)


class Ring:

    def __init__(self, nc, keep, sem, w_gu, w_dn):
        self.gu = keep("ring_gu", [P, HALF, DK, 2 * INNER])
        self.dn = keep("ring_dn", [IH, HALF, 2, D])
        self.lot_in = [sem(f"lot_in{n}") for n in range(HALF // LOT)]
        self.w_gu = w_gu.rearrange("e (c p) f -> p e c f", p=P)
        self.w_dn = w_dn.rearrange("e (p m) n -> p e m n", m=2)

    def load(self, eng, half, lot):
        a, e = lot * LOT, half * HALF + lot * LOT
        for k in range(LOT):
            eng.dma_start(self.gu[:, a + k, :, :], self.w_gu[:, e + k]).then_inc(self.lot_in[lot], 16)
        eng.dma_start(self.dn[:, a:a + LOT, :, :], self.w_dn[:, e:e + LOT]).then_inc(self.lot_in[lot], 16)

    LOADS = 16 * 5


def attention(nc, sem, X, identf, st2, ring, x, ctx_in, pos, wq, wkv, wout, bout):
    with ExitStack() as es:
        def sb(name, shape, dt=F32):
            return es.enter_context(nc.sbuf_tensor(name, shape, dt))

        POS = sb("POS", [P, NB, 2])
        WQ = sb("WQ", [P, DK, D])
        WKV = sb("WKV", [P, 2 * D])
        WO = sb("WO", [P, DK, D])
        BO = sb("BO", [P, D])
        identh = sb("identh", [P, P], F16)
        CT = [sb(f"CT{i}", [P, DC]) for i in range(2)]
        xn = sb("xn", [P, D])
        xcT = [sb(f"xcT{i}", [P, 3, P]) for i in range(2)]
        t1 = sb("t1", [P, 2 * D])
        t2 = sb("t2", [P, 2 * D])
        rot = sb("rot", [P, 2 * D])
        tokst = sb("tokst", [P, 2, NH, SLOT], F16)
        qst = [sb(f"qst{i}", [P, QUADS, P], F16) for i in range(2)]
        kT = sb("kT", [P, QUADS, P], F16)
        kz = [sb(f"kz{i}", [P, 4, QUADS, P], F16) for i in range(2)]
        V = [sb(f"V{i}", [P, NH, SLOT]) for i in range(2)]
        mx = [sb(f"mx{i}", [P, 2, 4], F16) for i in range(2)]
        mxs = [sb(f"mxs{i}", [8, P], F16) for i in range(2)]
        pw = [sb(f"pw{i}", [P, 4 * P]) for i in range(2)]
        OT = [sb(f"OT{i}", [P, 4, P]) for i in range(2)]
        rec = sb("rec", [P, 2, NH // 2])
        attn = sb("attn", [P, D])
        attnT = sb("attnT", [P, DK, P])
        st1 = sb("st1", [P, NB, 6])
        mv1 = sb("mv1", [P, NB, 2])
        rs1 = sb("rs1", [P, NB, 1])
        nb1 = sb("nb1", [P, NB, 1])
        ang = sb("ang", [P, 2, NB, 2, 2])
        turns = sb("turns", [P, 2, NB, 2, 2])
        RC = sb("RC", [P, NB, 4, 2])
        RS = sb("RS", [P, NB, 4, 2])
        bank = [es.enter_context(nc.psum_tensor(f"bank{i}", [P, 512], F32)) for i in range(8)]
        SB, STB, OB, M0, M1 = bank[0:2], bank[2:4], bank[4:6], bank[6], bank[7]

        x_in = [sem(f"x_in{i}") for i in range(4)]
        pos_in, w_in, bo_in = sem("pos_in"), sem("w_in"), sem("bo_in")
        ctx_in_s = [sem(f"ctx_in{i}") for i in range(2)]
        consts, consts2 = sem("consts"), sem("consts2")
        stat1, mv1_ok, std1, rs1_ok = sem("stat1"), sem("mv1_ok"), sem("std1"), sem("rs1_ok")
        turn_s, sin_s, rope_tab = sem("turn_s"), sem("sin_s"), sem("rope_tab")
        xn_ok, x_biased = sem("xn_ok"), sem("x_biased")
        xcT_mm, xcT_ok = sem("xcT_mm"), sem("xcT_ok")
        qk_mm, rope_ok, rot_ok, hi_ok, tokst_ok = sem("qk_mm"), sem("rope_ok"), sem("rot_ok"), sem("hi_ok"), sem("tokst_ok")
        qstT_mm, kstT_mm, qst_ok, kT_ok = sem("qstT_mm"), sem("kstT_mm"), sem("qst_ok"), sem("kT_ok")
        kz_in = [sem(f"kz_in{i}") for i in range(2)]
        v_mm, v_ok = sem("v_mm"), sem("v_ok")
        s_mm, max_ok, mxT_mm, mxs_ok = sem("s_mm"), sem("max_ok"), sem("mxT_mm"), sem("mxs_ok")
        mr_in = [sem(f"mr_in{i}") for i in range(2)]
        st_mm, exp_ok, pv_mm, OT_ok = sem("st_mm"), sem("exp_ok"), sem("pv_mm"), sem("OT_ok")
        ob_mm, rec_ok, attn_ok = sem("ob_mm"), sem("rec_ok"), sem("attn_ok")
        attnT_mm, attnT_ok, wo_mm, x1_ok, st2_ok = (sem(n) for n in ("attnT_mm", "attnT_ok", "wo_mm", "x1_ok", "st2_ok"))

        xr = x.rearrange("b p d -> p b d")

        def periods(eng, period):
            period(Batch(-1, 1))
            period(Batch(0, 0))
            period(Batch(0, 1))
            with eng.Fori(0, 6) as i:
                for u in range(2):
                    period(Batch(i, 2 + u))
            for n in (14, 15, 16):
                period(Batch(n // 2, n % 2))

        def inside(b, lo=0, hi=NB - 1):
            return not isinstance(b.n, int) or lo <= b.n <= hi

        block = es.enter_context(nc.Block())

        @block.sync
        def _(sp):
            sp.dma_start(POS[:, :, :], pos.rearrange("b p a -> p b a")).then_inc(pos_in, 16)
            for c in range(4):
                sp.dma_start(X[:, 4 * c:4 * c + 4, :], xr[:, 4 * c:4 * c + 4, :]).then_inc(x_in[c], 16)
                if c == 0:
                    sp.dma_start(CT[0][:, :], ctx_in[0]).then_inc(ctx_in_s[0], 16)
                    sp.dma_start(WQ[:, :, :], wq.rearrange("(c p) n -> p c n", p=P)).then_inc(w_in, 16)
                    sp.dma_start(WKV[:, :], wkv).then_inc(w_in, 16)
                    sp.dma_start(WO[:, :, :], wout.rearrange("(c p) n -> p c n", p=P)).then_inc(w_in, 16)
                    sp.dma_start(BO[:, :], bout.rearrange("(a n) -> a n", a=1).broadcast_to([P, D])).then_inc(bo_in, 16)
            sp.wait_ge(consts, 8)

            def period(b):
                m2 = b + 2
                if inside(m2):
                    at_least(sp, xcT_mm, b.n + 1)
                    sp.wait_ge(consts, 8)
                    sp.dma_start(CT[m2.par][:, :], ctx_in[m2.n]).then_inc(ctx_in_s[m2.par], 16)
                m1 = b + 1
                if inside(m1):
                    at_least(sp, kT_ok, m1.n + 1)
                    for j in range(4):
                        sp.dma_start(kz[m1.par][32 * j:32 * j + 32, j, :, :],
                                     kT[32 * j:32 * j + 32, :, :]).then_inc(kz_in[m1.par], 16)
                for g in (1, 3, 5, 7):
                    who, half = (b, (g + 3) // 2) if g < 5 else (m1, (g - 5) // 2)
                    if inside(who):
                        k = 4 * who.n + half
                        sp.wait_ge(mxs_ok, k + 1)
                        dst = qst[who.par][MAXROW:P:SLOT, 2 * half:2 * half + 2, :]
                        for q in range(2):
                            sp.dma_start(dst[:, q, :], mxs[half % 2][4 * q:4 * q + 4, :]).then_inc(mr_in[half % 2], 16)
            periods(sp, period)

        @block.gpsimd
        def _(pool):
            pool.memset(identf[:, :], 0.0).then_inc(consts, 1)
            pool.memset(identh[:, :], 0.0).then_inc(consts, 1)
            for i in range(2):
                pool.memset(kz[i][:, :, :, :], 0.0).then_inc(consts, 1)
                pool.memset(V[i][:, :, HD + 1:SLOT], 0.0).then_inc(consts, 1)
                pool.memset(V[i][:, :, HD:HD + 1], 1.0).then_inc(consts, 1)
            pool.wait_ge(consts, 2)
            for m in (identf, identh):
                pool.affine_select(out=m[:, :], in_=m[:, :], compare_op=ALU.not_equal, fill=1.0, base=0,
                                   pattern=[[-1, P]], channel_multiplier=1).then_inc(consts2, 1)
            pool.memset(tokst[:, :, :, MAXROW:SLOT], 0.0).then_inc(consts2, 1)
            pool.wait_ge(consts2, 3)
            pool.memset(tokst[:, 1, :, MAXROW:MAXROW + 1], 1.0).then_inc(consts2, 1)

            def split(m):
                at_least(pool, rope_ok, m.n + 1)
                at_least(pool, tokst_ok, 2 * m.n)
                pool.tensor_tensor(rot[:, :], t1[:, :], t2[:, :], ALU.add).then_inc(rot_ok, 1)
                pool.wait_ge(consts2, 4)
                at_least(pool, rot_ok, m.n + 1)
                at_least(pool, kstT_mm, m.n)
                r4 = rot[:, :].rearrange("p (w h d) -> p w h d", w=2, d=HD)
                pool.tensor_copy(tokst[:, :, :, 0:HD], r4).then_inc(hi_ok, 1)
                at_least(pool, hi_ok, m.n + 1)
                pool.wait_ge(consts2, 4)
                hi = tokst[:, :, :, 0:HD]
                for w in range(2):
                    a = (2 - w) * HD
                    pool.tensor_tensor(tokst[:, w, :, a:a + HD], r4[:, w], hi[:, w], ALU.subtract)
                    a = (1 + w) * HD
                    ins = pool.tensor_copy(tokst[:, w, :, a:a + HD], hi[:, w])
                    ins.then_inc(tokst_ok, 1)

            def add_bias(m):
                at_least(pool, xn_ok, m.n + 1)
                pool.tensor_tensor(X[:, m.n, :], X[:, m.n, :], BO[:, :], ALU.add).then_inc(x_biased, 1)

            pool.wait_ge(bo_in, 16)
            add_bias(Batch(0, 0))
            split(Batch(0, 0))

            def period(b):
                if inside(b + 2):
                    add_bias(b + 2)
                    split(b + 2)
            periods(pool, period)

        @block.scalar
        def _(act):
            for lot in range(HALF // LOT):
                ring.load(act, 0, lot)
            act.wait_ge(turn_s, 5)
            act.activation(ang[:, :, :, :, :], turns[:, :, :, :, :], ACT.Sin, scale=TWO_PI).then_inc(sin_s, 1)
            act.wait_ge(mv1_ok, 2)
            act.activation(rs1[:, :, 0], nb1[:, :, 0], ACT.Sqrt).then_inc(std1, 1)

            def norm(m):
                act.wait_ge(rs1_ok, 2)
                at_least(act, xcT_mm, m.n)
                act.activation(xn[:, :], X[:, m.n, :], ACT.Identity, bias=nb1[:, m.n, :],
                               scale=rs1[:, m.n, :]).then_inc(xn_ok, 1)

            def evac_xcT(m):
                at_least(act, xcT_mm, m.n + 1)
                at_least(act, v_mm, m.n - 1)
                act.copy(xcT[m.par][:, :, :], M1[:, 0:3 * P].rearrange("p (c t) -> p c t", c=3)).then_inc(xcT_ok, 1)

            norm(Batch(0, 0))
            evac_xcT(Batch(0, 0))

            def period(b):
                m1, m2, o = b + 1, b + 2, b + -1
                for g in range(QUADS):
                    if inside(b):
                        act.wait_ge(st_mm, QUADS * b.n + g + 1)
                        at_least(act, pv_mm, QUADS * b.n + g - 1)
                        act.activation(pw[g % 2][:, :], STB[g % 2][:, :], ACT.Exp, scale=SCALE).then_inc(exp_ok, 1)
                    if g == 0 and inside(m1):
                        at_least(act, qstT_mm, m1.n + 1)
                        at_least(act, st_mm, QUADS * b.n)
                        act.copy(qst[m1.par][:, :, :], M0[:, :].bitcast(F16).rearrange("p (q t) -> p q t", q=QUADS)).then_inc(qst_ok, 1)
                    if g == 1:
                        if inside(m1):
                            at_least(act, kstT_mm, m1.n + 1)
                            if inside(b):
                                act.wait_ge(kz_in[b.par], 64 * (b.half + 1))
                            act.copy(kT[:, :, :], M1[:, :].bitcast(F16).rearrange("p (q t) -> p q t", q=QUADS)).then_inc(kT_ok, 1)
                        if inside(m2):
                            norm(m2)
                        if inside(o):
                            evac_OT(o, 1)
                    if g == 3 and inside(m2):
                        evac_xcT(m2)
                    if g == 4 and inside(m1):
                        at_least(act, v_mm, m1.n + 1)
                        at_least(act, pv_mm, QUADS * b.n)
                        act.copy(V[m1.par][:, :, 0:HD], M0[:, 0:D].rearrange("p (h d) -> p h d", d=HD)).then_inc(v_ok, 1)
                    if g == 5 and inside(b):
                        evac_OT(b, 0)
                    if g == 6 and inside(o):
                        act.wait_ge(attnT_mm, o.n + 1)
                        at_least(act, wo_mm, o.n)
                        act.copy(attnT[:, :, :], M0[:, D:2 * D].rearrange("p (c t) -> p c t", c=DK)).then_inc(attnT_ok, 1)

            def evac_OT(m, half):
                act.wait_ge(pv_mm, QUADS * m.n + 4 * half + 4)
                at_least(act, ob_mm, 2 * m.n + half - 1)
                act.copy(OT[half][:, :, :], OB[half][:, :].rearrange("p (q t) -> p q t", q=4)).then_inc(OT_ok, 1)
            periods(act, period)

        @block.vector
        def _(dve):
            freq = [float(np.float32(10000.0) ** np.float32(-f / 2)) for f in range(2)]
            dve.wait_ge(pos_in, 16)
            for f in range(2):
                for c in range(2):
                    dve.tensor_scalar(turns[:, c, :, :, f], POS[:, :, :], freq[f] / (2 * np.pi), 0.25 * c,
                                      ALU.mult, ALU.add).then_inc(turn_s, 1)
            dve.wait_ge(turn_s, 4)
            dve.tensor_scalar(ang[:, :, :, :, :], turns[:, :, :, :, :], BIG, BIG, ALU.add, ALU.subtract).then_inc(rope_tab, 1)
            dve.wait_ge(rope_tab, 1)
            dve.tensor_tensor(turns[:, :, :, :, :], turns[:, :, :, :, :], ang[:, :, :, :, :], ALU.subtract).then_inc(turn_s, 1)
            for c in range(4):
                dve.wait_ge(x_in[c], 16)
                for j in range(4 * c, 4 * c + 4):
                    dve.bn_stats(st1[:, j, :], X[:, j, :]).then_inc(stat1, 1)
            for j in range(NB):
                dve.wait_ge(stat1, j + 1)
                ins = dve.bn_aggr(mv1[:, j, :], st1[:, j, :])
            ins.then_inc(mv1_ok, 1)
            dve.wait_ge(mv1_ok, 1)
            dve.tensor_scalar(nb1[:, :, 0], mv1[:, :, 1], EPS, None, ALU.add).then_inc(mv1_ok, 1)
            dve.wait_ge(sin_s, 1)
            sin = ang[:, 0].rearrange("p b a f -> p b (a f)")
            cos = ang[:, 1].rearrange("p b a f -> p b (a f)")
            for r in range(2):
                dve.tensor_copy(RC[:, :, :, r], cos)
                dve.tensor_scalar(RS[:, :, :, r], sin, -1.0 if r == 0 else 1.0, None, ALU.mult).then_inc(rope_tab, 1)
            dve.wait_ge(std1, 1)
            dve.reciprocal(rs1[:, :, 0], rs1[:, :, 0]).then_inc(rs1_ok, 1)
            dve.wait_ge(rs1_ok, 1)
            dve.scalar_tensor_tensor(out=nb1[:, :, 0], in0=mv1[:, :, 0], scalar=-1.0, in1=rs1[:, :, 0],
                                     op0=ALU.mult, op1=ALU.mult).then_inc(rs1_ok, 1)
            dve.wait_ge(rope_tab, 3)

            def rope(m):
                at_least(dve, qk_mm, m.n + 1)
                at_least(dve, rot_ok, m.n)
                qk = M1[:, :].rearrange("p (x a r) -> p x a r", a=4, r=2)
                o1 = t1[:, :].rearrange("p (x a) -> p x a", a=8)
                o2 = t2[:, :].rearrange("p (x a r) -> p x a r", a=4, r=2)
                rc = RC[:, m.n].rearrange("p a r -> p (a r)").unsqueeze(1).broadcast_to([P, 2 * NH, 8])
                dve.tensor_tensor(o1, M1[:, :].rearrange("p (x a) -> p x a", a=8), rc, ALU.mult)
                for r in range(2):
                    rs = RS[:, m.n, :, r].unsqueeze(1).broadcast_to([P, 2 * NH, 4])
                    ins = dve.tensor_tensor(o2[:, :, :, r], qk[:, :, :, 1 - r], rs, ALU.mult)
                ins.then_inc(rope_ok, 1)

            rope(Batch(0, 0))

            def row_max(m, u):
                dve.wait_ge(s_mm, QUADS * m.n + u + 1)
                if not (isinstance(m.n, int) and 4 * m.n + u // 2 < 2):
                    dve.wait_ge(mxT_mm, 4 * m.n + u // 2 - 1)
                dve.tensor_reduce(mx[u // 2 % 2][:, u % 2, :], SB[u % 2][:, :].rearrange("p (j t) -> p j t", j=4),
                                  axis=AX.X, op=ALU.max, negate=True).then_inc(max_ok, 1)

            def evac_max(m, half):
                k = 4 * m.n + half
                dve.wait_ge(mxT_mm, k + 1)
                at_least(dve, mr_in[half % 2], 32 * (2 * m.n + half // 2))
                dve.tensor_copy(mxs[half % 2][:, :], SB[1][0:8, 0:P // 2].bitcast(F16)).then_inc(mxs_ok, 1)

            def normalise(m, half):
                at_least(dve, ob_mm, 2 * m.n + half + 1)
                ob = OB[half][:, :].rearrange("p (h s) -> p h s", s=SLOT)
                at_least(dve, attn_ok, 2 * m.n + half)
                dve.reciprocal(rec[:, half, :], ob[:, :, HD]).then_inc(rec_ok, 1)
                at_least(dve, attnT_mm, m.n)
                dve.wait_ge(rec_ok, 2 * m.n + half + 1)
                dve.tensor_tensor(attn[:, half * P:half * P + P].rearrange("p (h d) -> p h d", d=HD), ob[:, :, 0:HD],
                                  rec[:, half, :].unsqueeze(2).broadcast_to([P, NH // 2, HD]), ALU.mult).then_inc(attn_ok, 1)

            def period(b):
                m1, m2, o = b + 1, b + 2, b + -1
                for g in range(QUADS):
                    who, u = (b, g + 5) if g < 3 else (m1, g - 3)
                    if inside(who):
                        row_max(who, u)
                    if g % 2 == 1:
                        who, half = (b, (g + 3) // 2) if g < 5 else (m1, (g - 5) // 2)
                        if inside(who):
                            evac_max(who, half)
                    if g == 0 and inside(o):
                        normalise(o, 0)
                    if g == 3 and inside(o):
                        normalise(o, 1)
                    if g == 5 and inside(m2):
                        rope(m2)
                    if g == 7 and inside(o):
                        dve.wait_ge(wo_mm, o.n + 1)
                        dve.wait_ge(x_biased, o.n + 1)
                        dve.tensor_tensor(X[:, o.n, :], M0[:, 0:D], X[:, o.n, :], ALU.add).then_inc(x1_ok, 1)
                        dve.wait_ge(x1_ok, o.n + 1)
                        dve.wait_ge(rope_tab, 3)
                        dve.bn_stats(st2[:, o.n, :], X[:, o.n, :]).then_inc(st2_ok, 1)
            periods(dve, period)

        @block.tensor
        def _(pe):
            pe.wait_ge(consts2, 4)
            pe.wait_ge(consts, 8)

            def transpose_xc(m):
                at_least(pe, xn_ok, m.n + 1)
                pe.wait_ge(ctx_in_s[m.par], 16 * (m.half + 1))
                at_least(pe, kT_ok, m.n - 1)
                for c in range(DK):
                    pe.transpose(M1[:, c * P:c * P + P], xn[:, c * P:c * P + P], identf[:, :])
                pe.transpose(M1[:, DK * P:DK * P + P], CT[m.par][:, :], identf[:, :]).then_inc(xcT_mm, 1)

            def project_qk(m):
                at_least(pe, xcT_ok, m.n + 1)
                for c in range(DK):
                    pe.matmul(M1[:, 0:D], xcT[m.par][:, c, :], WQ[:, c, :], start=(c == 0), stop=(c == DK - 1))
                pe.matmul(M1[:, D:2 * D], xcT[m.par][:, DK, :], WKV[:, 0:D], start=True, stop=True).then_inc(qk_mm, 1)

            def transpose_stacks(m):
                at_least(pe, tokst_ok, 2 * m.n + 2)
                at_least(pe, v_ok, m.n)
                at_least(pe, x1_ok, m.n - 2)
                for q in range(QUADS):
                    ins = pe.transpose(M0[:, q * 64:q * 64 + 64].bitcast(F16), tokst[:, 0, 4 * q:4 * q + 4, :], identh[:, :])
                ins.then_inc(qstT_mm, 1)
                at_least(pe, rope_ok, m.n + 1)
                for q in range(QUADS):
                    ins = pe.transpose(M1[:, q * 64:q * 64 + 64].bitcast(F16), tokst[:, 1, 4 * q:4 * q + 4, :], identh[:, :])
                ins.then_inc(kstT_mm, 1)

            def project_v(m):
                at_least(pe, qst_ok, m.n + 1)
                pe.matmul(M0[:, 0:D], xcT[m.par][:, DK, :], WKV[:, D:2 * D], start=True, stop=True).then_inc(v_mm, 1)

            def logits_q(m, u):
                if u == 0:
                    at_least(pe, qst_ok, m.n + 1)
                    pe.wait_ge(kz_in[m.par], 64 * (m.half + 1))
                at_least(pe, max_ok, QUADS * m.n + u - 1)
                if u % 2:
                    at_least(pe, mxs_ok, 4 * m.n + u // 2)
                pe.matmul(SB[u % 2][:, :], qst[m.par][:, u, :], kz[m.par][:, :, u, :], start=True, stop=True).then_inc(s_mm, 1)

            def transpose_max(m, half):
                pe.wait_ge(max_ok, QUADS * m.n + 2 * half + 2)
                pe.transpose(SB[1][0:8, 0:P // 2].bitcast(F16), mx[half % 2][:, :, :], identh[:, :]).then_inc(mxT_mm, 1)

            def logits_k(m, g):
                at_least(pe, exp_ok, QUADS * m.n + g - 1)
                if g % 2 == 0:
                    half = g // 2
                    pe.wait_ge(mr_in[half % 2], 32 * (2 * m.n + half // 2 + 1))
                for j in range(4):
                    ins = pe.matmul(STB[g % 2][:, j * P:j * P + P], kz[m.par][:, j, g, :], qst[m.par][:, g, :],
                                    start=True, stop=True)
                ins.then_inc(st_mm, 1)

            def weigh_values(m, g):
                pe.wait_ge(exp_ok, QUADS * m.n + g + 1)
                if g == 0:
                    at_least(pe, v_ok, m.n + 1)
                if g % 4 == 0:
                    at_least(pe, attn_ok, 2 * m.n + g // 4 - 1)
                for j in range(4):
                    ins = pe.matmul(OB[g // 4][32 * j:32 * j + 32, (g % 4) * P:(g % 4) * P + P], V[m.par][:, 4 * g + j, :],
                                    pw[g % 2][:, j * P:j * P + P], start=True, stop=True, tile_position=(0, 32 * j))
                ins.then_inc(pv_mm, 1)

            def transpose_outputs(m, half):
                pe.wait_ge(OT_ok, 2 * m.n + half + 1)
                for q in range(4):
                    ins = pe.transpose(OB[half][:, q * P:q * P + P], OT[half][:, q, :], identf[:, :])
                ins.then_inc(ob_mm, 1)

            def transpose_attn(m):
                pe.wait_ge(attn_ok, 2 * m.n + 2)
                pe.wait_ge(v_ok, min(m.n + 3, NB) if isinstance(m.n, int) else m.n + 3)
                for c in range(DK):
                    ins = pe.transpose(M0[:, D + c * P:D + c * P + P], attn[:, c * P:c * P + P], identf[:, :])
                ins.then_inc(attnT_mm, 1)

            def project_out(m):
                pe.wait_ge(attnT_ok, m.n + 1)
                for c in range(DK):
                    ins = pe.matmul(M0[:, 0:D], attnT[:, c, :], WO[:, c, :], start=(c == 0), stop=(c == DK - 1))
                ins.then_inc(wo_mm, 1)

            pe.wait_ge(w_in, 48)
            transpose_xc(Batch(0, 0))
            project_qk(Batch(0, 0))

            def period(b):
                m1, m2, o = b + 1, b + 2, b + -1
                for g in range(QUADS):
                    if inside(b):
                        logits_k(b, g)
                    who, u = (b, g + 5) if g < 3 else (m1, g - 3)
                    if inside(who):
                        logits_q(who, u)
                    if g % 2 == 1:
                        who, half = (b, (g + 3) // 2) if g < 5 else (m1, (g - 5) // 2)
                        if inside(who):
                            transpose_max(who, half)
                    if g == 0 and inside(o):
                        weigh_values(o, QUADS - 1)
                    if g > 0 and inside(b):
                        weigh_values(b, g - 1)
                    if g == 0 and inside(m1):
                        transpose_stacks(m1)
                    if g == 2:
                        if inside(m2):
                            transpose_xc(m2)
                        if inside(o):
                            transpose_outputs(o, 1)
                    if g == 3 and inside(m1):
                        project_v(m1)
                    if g == 4 and inside(m2):
                        project_qk(m2)
                    if g == 5 and inside(o):
                        transpose_attn(o)
                    if g == 7:
                        if inside(o):
                            project_out(o)
                        if inside(b):
                            transpose_outputs(b, 0)
            periods(pe, period)


def mixture(nc, sem, X, identf, st2, ring, gate_w, ws_gu, ws_dn, out):
    G4, R = 4, CAP // 4
    FC = [(0, 128), (128, 128), (256, SHARED - 256)]
    ROW = D + NE
    with ExitStack() as es:
        def sb(name, shape, dt=F32):
            return es.enter_context(nc.sbuf_tensor(name, shape, dt))

        table = nc.dram_tensor("table", (T, ROW), F32, kind="Internal").ap()
        hT = sb("hT", [P, DK, T])
        h = [sb(f"h{i}", [P, D]) for i in range(2)]
        mv2 = sb("mv2", [P, NB, 2])
        rs2 = sb("rs2", [P, NB])
        nb2 = sb("nb2", [P, NB])
        gw = sb("gw", [NE, D])
        gwT = sb("gwT", [P, DK, NE])
        WSG = sb("WSG", [P, DK, 2 * SHARED])
        WSD = sb("WSD", [P, 3, D])
        zero = sb("zero", [CAP, D])
        gm = sb("gm", [P, NB, GROUPS])
        gv = sb("gv", [P, NB, 8])
        gi = sb("gi", [P, NB, 8], U32)
        gif = sb("gif", [P, NB, 8])
        io8 = sb("io8", [P, GROUPS])
        kp = [sb(f"kp{i}", [P, NB, GROUPS]) for i in range(TOPG)]
        sc = sb("sc", [P, NB, NE])
        ex = sb("ex", [P, NB, NE])
        wt = sb("wt", [P, NB, NE])
        smx = sb("smx", [P, NB])
        ssum = sb("ssum", [P, NB])
        ei = sb("ei", [P, NB, 8], U32)
        eih = sb("eih", [P, NB, 8], F16)
        io32 = sb("io32", [P, NE], F16)
        eq = [sb(f"eq{i}", [P, NB, NE], F16) for i in range(2)]
        chosen = sb("chosen", [P, NB, NE], F16)
        chosen4 = sb("chosen4", [P, NB, G4, NE], F16)
        tri = sb("tri", [P, 4 * P], F16)
        ones4 = sb("ones4", [P, 4 * P], F16)
        cum = sb("cum", [P, T], F16)
        junk = sb("junk", [P, T], F16)
        junk2 = sb("junk2", [P, T], F16)
        thr = sb("thr", [P, R])
        thr_half = sb("thr_half", [P, R])
        tok = sb("tok", [P, R])
        toki = sb("toki", [P, R], U32)
        own = sb("own", [P, NE])
        io48 = sb("io48", [P, CAP])
        place = sb("place", [P, R, CAP])
        tw = sb("tw", [P, R, 2, NE])
        xg = sb("xg", [P, R, ROW])
        xbT = sb("xbT", [P, DK, NE, CAP])
        pcol = sb("pcol", [CAP, 1])
        tw48 = sb("tw48", [CAP, 2, NE])
        inv = sb("inv", [CAP, NE])
        dst = sb("dst", [CAP, NE], U32)
        sg = [sb(f"sg{i}", [P, 512]) for i in range(2)]
        ac = [sb(f"ac{i}", [P, 3, 512]) for i in range(2)]
        ro = [sb(f"ro{i}", [P, D]) for i in range(2)]
        es_ = [sb(f"es{i}", [IH, 2, CAP]) for i in range(2)]
        ea = [sb(f"ea{i}", [IH, 2, CAP]) for i in range(2)]
        ys = [sb(f"ys{i}", [CAP, D]) for i in range(3)]
        ix = [sb(f"ix{i}", [CAP, 1], U32) for i in range(3)]
        bank = [es.enter_context(nc.psum_tensor(f"mbank{i}", [P, 512], F32)) for i in range(8)]
        GU, DN, TB, LG = bank[0:4], bank[4], bank[5:7], bank[7]
        EB, YB = bank[0:3], bank[3:5]

        w2_in, gw_in, zero_ok, zero_in = sem("w2_in"), sem("gw_in"), sem("zero_ok"), sem("zero_in")
        mc_ok, mc2_ok = sem("mc_ok"), sem("mc2_ok")
        mv2_ok, std2, rs2_ok = sem("mv2_ok"), sem("std2"), sem("rs2_ok")
        h_ok, h_in, hT_mm, hT_ok = sem("h_ok"), [sem(f"h_in{i}") for i in range(2)], sem("hT_mm"), sem("hT_ok")
        gwT_mm, gwT_ok, lg_mm = sem("gwT_mm"), sem("gwT_ok"), sem("lg_mm")
        route, sc_ok, ex_ok, wt_ok, wt_in = sem("route"), sem("sc_ok"), sem("ex_ok"), sem("wt_ok"), sem("wt_in")
        chosen_ok, cum_mm, cum_ok = sem("chosen_ok"), sem("cum_mm"), sem("cum_ok")
        cnt_act, cnt_ok, toki_ok, xg_in = sem("cnt_act"), sem("cnt_ok"), sem("toki_ok"), [sem(f"xg_in{r}") for r in range(R)]
        tw_ok, tw_mm, tw48_ok, dst_ok = sem("tw_ok"), sem("tw_mm"), sem("tw48_ok"), sem("dst_ok")
        xb_mm, xb_ok = sem("xb_mm"), sem("xb_ok")
        up_mm, sg_ok, ac_ok, dn_mm, ro_ok = sem("up_mm"), sem("sg_ok"), sem("ac_ok"), sem("dn_mm"), sem("ro_ok")
        ro_in = [sem(f"ro_in{i}") for i in range(2)]
        eup_mm, es_ok, ea_ok, y_mm, ys_ok, ix_ok, add_in = (sem(n) for n in ("eup_mm", "es_ok", "ea_ok", "y_mm", "ys_ok", "ix_ok", "add_in"))

        block = es.enter_context(nc.Block())

        @block.sync
        def _(sp):
            sp.dma_start(gw[:, :], gate_w).then_inc(gw_in, 16)
            sp.dma_start(WSG[:, :, :], ws_gu.rearrange("(c p) f -> p c f", p=P)).then_inc(w2_in, 16)
            sp.dma_start(WSD[:, 0:2, :], ws_dn[0:256].rearrange("(c p) n -> p c n", p=P)).then_inc(w2_in, 16)
            sp.dma_start(WSD[0:FC[2][1], 2, :], ws_dn[256:SHARED]).then_inc(w2_in, 16)
            sp.wait_ge(zero_ok, 1)
            sp.dma_start(out[T:T + CAP, :], zero[:, :]).then_inc(zero_in, 16)
            for m in range(NB):
                sp.wait_ge(h_ok, m + 1)
                sp.dma_start(table[m * P:m * P + P, 0:D], h[m % 2][:, :]).then_inc(h_in[m % 2], 16)
            for m in range(NB):
                if m == 4:
                    sp.wait_ge(wt_ok, 1)
                    sp.dma_start(table[:, D:ROW].rearrange("(b p) e -> p b e", p=P), wt[:, :, :]).then_inc(wt_in, 16)
                sp.wait_ge(ro_ok, m + 1)
                sp.dma_start(out[m * P:m * P + P, :], ro[m % 2][:, :]).then_inc(ro_in[m % 2], 16)
            for lot in range(HALF // LOT):
                sp.wait_ge(y_mm, LOT * (lot + 1))
                ring.load(sp, 1, lot)

        @block.gpsimd
        def _(pool):
            pool.memset(zero[:, :], 0.0).then_inc(zero_ok, 1)
            pool.memset(tri[:, :], 1.0).then_inc(mc_ok, 1)
            pool.memset(ones4[:, :], 1.0).then_inc(mc2_ok, 1)
            pool.wait_ge(mc_ok, 1)
            pool.affine_select(out=tri[:, 0:P], in_=tri[:, 0:P], compare_op=ALU.is_ge, fill=0.0, base=0,
                               pattern=[[1, P]], channel_multiplier=-1).then_inc(mc2_ok, 1)
            pool.iota(io8[:, :], [[1, GROUPS]], base=0, channel_multiplier=0, allow_small_or_imprecise_dtypes=True).then_inc(mc2_ok, 1)
            pool.iota(io32[:, :], [[1, NE]], base=0, channel_multiplier=0, allow_small_or_imprecise_dtypes=True).then_inc(mc2_ok, 1)
            pool.iota(io48[:, :], [[1, CAP]], base=0, channel_multiplier=0, allow_small_or_imprecise_dtypes=True).then_inc(mc2_ok, 1)
            pool.iota(pcol[:, :], [[0, 1]], base=0, channel_multiplier=1, allow_small_or_imprecise_dtypes=True).then_inc(mc2_ok, 1)
            for g in range(G4):
                rows = slice(NE * g, NE * g + NE)
                pool.wait_ge(mc2_ok, 6 + 2 * g)
                pool.iota(thr[rows, :], [[1, R]], base=R * g, channel_multiplier=0, allow_small_or_imprecise_dtypes=True).then_inc(mc2_ok, 1)
                pool.iota(own[rows, :], [[1, NE]], base=0, channel_multiplier=-1, allow_small_or_imprecise_dtypes=True).then_inc(mc2_ok, 1)
            for r in range(R):
                if r == 0:
                    pool.wait_ge(toki_ok, 1)
                    for i in range(2):
                        pool.wait_ge(h_in[i], 16 * (NB // 2))
                    pool.wait_ge(wt_in, 16)
                pool.indirect_dma_start(xg[:, r, :], None, table[:, :], bass.IndirectOffsetOnAxis(ap=toki[:, r:r + 1], axis=0)
                                        ).then_inc(xg_in[r], 16)
            pool.wait_ge(zero_in, 16)
            for i in range(2):
                pool.wait_ge(ro_in[i], 16 * (NB // 2))

            def add(e, s):
                pool.wait_ge(ys_ok, e + 1)
                pool.wait_ge(ix_ok, e + 1)
                at_least(pool, add_in, 16 * e)
                pool.indirect_dma_start(out[:, :], bass.IndirectOffsetOnAxis(ap=ix[s % 3][:, 0:1], axis=0), ys[s % 3][:, :], None,
                                        compute_op=ALU.add).then_inc(add_in, 16)
            for e in range(NE):
                add(e, e)
            pool.wait_ge(add_in, 16 * NE)

        @block.scalar
        def _(act):
            act.wait_ge(mv2_ok, 2)
            act.activation(rs2[:, :], nb2[:, :], ACT.Sqrt).then_inc(std2, 1)
            act.wait_ge(gwT_mm, 1)
            act.copy(gwT[:, :, :], TB[0][:, 0:DK * NE].rearrange("p (c e) -> p c e", c=DK)).then_inc(gwT_ok, 1)
            act.wait_ge(rs2_ok, 2)
            for m in range(NB):
                at_least(act, hT_mm, m - 1)
                at_least(act, h_in[m % 2], 16 * (m // 2))
                act.activation(h[m % 2][:, :], X[:, m, :], ACT.Identity, bias=nb2[:, m:m + 1],
                               scale=rs2[:, m:m + 1]).then_inc(h_ok, 1)

            def gate(k, f):
                c, n = 3 * k + f, FC[f][1]
                act.wait_ge(up_mm, c + 1)
                at_least(act, ac_ok, c - 1)
                act.activation(sg[c % 2][0:n, :], GU[2 * (c % 2)][0:n, :], ACT.Silu).then_inc(sg_ok, 1)
            for f in range(3):
                gate(0, f)
            act.wait_ge(sc_ok, 1)
            act.activation(ex[:, :, :], sc[:, :, :], ACT.Exp).then_inc(ex_ok, 1)
            for k in range(1, 4):
                for f in range(3):
                    gate(k, f)
                if k == 2:
                    act.wait_ge(cum_ok, 4)
                    act.wait_ge(cnt_ok, 1)
                    for r in range(R - COUNT_ACT, R):
                        if r > R - COUNT_ACT:
                            act.wait_ge(cnt_act, r - (R - COUNT_ACT))
                        act.activation(junk2[:, :], cum[:, :], ACT.Sign, bias=thr_half[:, r:r + 1], scale=-1.0,
                                       accum_out=tok[:, r:r + 1]).then_inc(cnt_act, 1)
            for r in range(R):
                act.wait_ge(xb_mm, r + 1)
                for c in range(DK):
                    ins = act.copy(xbT[:, c, :, :].rearrange("p e (g r) -> p r g e", g=G4)[:, r],
                                   TB[r % 2][:, c * P:c * P + P].rearrange("p (g e) -> p g e", g=G4))
                ins.then_inc(xb_ok, 1)
            for e in range(NE):
                act.wait_ge(eup_mm, e + 1)
                at_least(act, ea_ok, e - 1)
                act.activation(es_[e % 2][:, :, :], EB[e % 3][0:IH, 0:2 * CAP].rearrange("p (m q) -> p m q", m=2), ACT.Silu).then_inc(es_ok, 1)

        @block.vector
        def _(dve):
            done = [0]

            def step(ins):
                done[0] += 1
                ins.then_inc(route, 1)
                dve.wait_ge(route, done[0])

            for m in range(NB):
                ins = dve.bn_aggr(mv2[:, m, :], st2[:, m, :])
            ins.then_inc(mv2_ok, 1)
            dve.wait_ge(mv2_ok, 1)
            dve.tensor_scalar(nb2[:, :], mv2[:, :, 1], EPS, None, ALU.add).then_inc(mv2_ok, 1)
            dve.wait_ge(std2, 1)
            dve.reciprocal(rs2[:, :], rs2[:, :]).then_inc(rs2_ok, 1)
            dve.wait_ge(rs2_ok, 1)
            dve.scalar_tensor_tensor(out=nb2[:, :], in0=mv2[:, :, 0], scalar=-1.0, in1=rs2[:, :],
                                     op0=ALU.mult, op1=ALU.mult).then_inc(rs2_ok, 1)
            for m in range(NB):
                dve.wait_ge(hT_mm, m + 1)
                dve.tensor_copy(hT[:, :, m * P:m * P + P], TB[m % 2][:, 0:D].rearrange("p (c t) -> p c t", c=DK)).then_inc(hT_ok, 1)

            def gated(k, f):
                c, n = 3 * k + f, FC[f][1]
                dve.wait_ge(sg_ok, c + 1)
                at_least(dve, dn_mm, 4 * (k - 1))
                dve.tensor_tensor(ac[k % 2][0:n, f, :], GU[2 * (c % 2) + 1][0:n, :], sg[c % 2][0:n, :], ALU.mult).then_inc(ac_ok, 1)

            def residual(m):
                dve.wait_ge(dn_mm, m + 1)
                at_least(dve, ro_in[m % 2], 16 * (m // 2))
                dve.tensor_tensor(ro[m % 2][:, :], DN[:, 0:D], X[:, m, :], ALU.add).then_inc(ro_ok, 1)

            dve.wait_ge(lg_mm, NB)
            dve.wait_ge(mc2_ok, 6 + 2 * G4)
            lg = LG[:, :].rearrange("p (b g k) -> p b g k", b=NB, g=GROUPS)
            step(dve.tensor_reduce(gm[:, :, :], lg, axis=AX.X, op=ALU.max))
            for m in range(NB):
                ins = dve.max(gv[:, m, :], gm[:, m, :])
            step(ins)
            for m in range(NB):
                ins = dve.max_index(gi[:, m, :], gv[:, m, :], gm[:, m, :])
            step(ins)
            gated(0, 0)
            step(dve.tensor_copy(gif[:, :, :], gi[:, :, :]))
            for k in range(TOPG):
                ins = dve.tensor_tensor(kp[k][:, :, :], io8[:, :].unsqueeze(1).broadcast_to([P, NB, GROUPS]),
                                        gif[:, :, k].unsqueeze(2).broadcast_to([P, NB, GROUPS]), ALU.is_equal)
            step(ins)
            step(dve.tensor_tensor(kp[0][:, :, :], kp[0][:, :, :], kp[1][:, :, :], ALU.add))
            step(dve.tensor_tensor(kp[0][:, :, :], kp[0][:, :, :], kp[2][:, :, :], ALU.add))
            step(dve.tensor_tensor(sc[:, :, :].rearrange("p b (g k) -> p b g k", g=GROUPS), lg,
                                   kp[0][:, :, :].unsqueeze(3).broadcast_to([P, NB, GROUPS, NE // GROUPS]), ALU.mult))
            step(dve.tensor_reduce(smx[:, :], sc[:, :, :], axis=AX.X, op=ALU.max))
            dve.tensor_tensor(sc[:, :, :], sc[:, :, :], smx[:, :].unsqueeze(2).broadcast_to([P, NB, NE]), ALU.subtract).then_inc(sc_ok, 1)
            gated(0, 1)
            gated(0, 2)
            dve.wait_ge(ex_ok, 1)
            step(dve.tensor_reduce(ssum[:, :], ex[:, :, :], axis=AX.X, op=ALU.add))
            step(dve.reciprocal(smx[:, :], ssum[:, :]))
            dve.scalar_tensor_tensor(out=wt[:, :, :], in0=ex[:, :, :], scalar=ROUTE_SCALE,
                                     in1=smx[:, :].unsqueeze(2).broadcast_to([P, NB, NE]), op0=ALU.mult, op1=ALU.mult).then_inc(wt_ok, 1)
            for m in range(4):
                residual(m)
            for m in range(NB):
                ins = dve.max(gv[:, m, :], ex[:, m, :])
            step(ins)
            for m in range(NB):
                ins = dve.max_index(ei[:, m, :], gv[:, m, :], ex[:, m, :])
            step(ins)
            gated(1, 0)
            step(dve.tensor_copy(eih[:, :, :], ei[:, :, :]))
            for k in range(TOPK):
                to = chosen if k == 0 else eq[k % 2]
                step(dve.tensor_tensor(to[:, :, :], io32[:, :].unsqueeze(1).broadcast_to([P, NB, NE]),
                                       eih[:, :, k].unsqueeze(2).broadcast_to([P, NB, NE]), ALU.is_equal))
                if k:
                    step(dve.tensor_tensor(chosen[:, :, :], chosen[:, :, :], to[:, :, :], ALU.add))
            for g in range(G4):
                ins = dve.tensor_copy(chosen4[:, :, g, :], chosen[:, :, :])
            ins.then_inc(chosen_ok, 1)
            gated(1, 1)
            gated(1, 2)
            step(dve.tensor_scalar(own[:, :], own[:, :], 0.0, None, ALU.is_equal))
            step(dve.tensor_tensor(place[:, :, :], io48[:, :].unsqueeze(1).broadcast_to([P, R, CAP]),
                                   thr[:, :].unsqueeze(2).broadcast_to([P, R, CAP]), ALU.is_equal))
            dve.tensor_scalar(thr_half[:, :], thr[:, :], 0.5, None, ALU.add).then_inc(cnt_ok, 1)
            for c in range(4):
                dve.wait_ge(cum_mm, c + 1)
                dve.tensor_copy(cum[:, 512 * c:512 * c + 512], TB[c % 2][:, :]).then_inc(cum_ok, 1)
            for m in range(4, 8):
                residual(m)
            dve.wait_ge(cum_ok, 4)

            def count(r):
                step(dve.tensor_scalar(junk[:, :], cum[:, :], thr[:, r:r + 1], None, ALU.is_le, ALU.add,
                                       accum_out=tok[:, r:r + 1]))
            n = R - COUNT_ACT
            for f in range(3):
                for r in range(f * n // 3, (f + 1) * n // 3):
                    count(r)
                gated(2, f)
            dve.wait_ge(cnt_act, COUNT_ACT)
            step(dve.tensor_scalar(tok[:, n:R], tok[:, n:R], 0.5, T / 2, ALU.mult, ALU.add))
            dve.tensor_scalar(toki[:, :], tok[:, :], float(T - 1), None, ALU.min).then_inc(toki_ok, 1)
            own_r = own[:, :].unsqueeze(1).broadcast_to([P, R, NE])
            dve.tensor_tensor(tw[:, :, 0, :], own_r, tok[:, :].unsqueeze(2).broadcast_to([P, R, NE]), ALU.mult)
            for m in range(8, 12):
                residual(m)
            for f in range(3):
                gated(3, f)
            for m in range(12, 16):
                residual(m)
            for r in range(R):
                dve.wait_ge(xg_in[r], 16)
            dve.tensor_tensor(tw[:, :, 1, :], own_r, xg[:, :, D:ROW], ALU.mult).then_inc(tw_ok, 1)
            dve.wait_ge(tw_mm, 1)
            dve.tensor_copy(tw48[:, :, :], LG[0:CAP, 0:2 * NE].rearrange("p (a e) -> p a e", a=2)).then_inc(tw48_ok, 1)
            dve.wait_ge(tw48_ok, 1)
            step(dve.tensor_scalar(inv[:, :], tw48[:, 0, :], float(T), pcol[:, :], ALU.is_ge, ALU.mult))
            dve.tensor_tensor(dst[:, :], inv[:, :], tw48[:, 0, :], ALU.add).then_inc(dst_ok, 1)
            dve.wait_ge(dst_ok, 1)

            def weighted(e):
                dve.wait_ge(y_mm, e + 1)
                at_least(dve, add_in, 16 * (e - 2))
                dve.tensor_copy(ix[e % 3][:, :], dst[:, e:e + 1]).then_inc(ix_ok, 1)
                dve.tensor_scalar(ys[e % 3][:, :], YB[e % 2][0:CAP, 0:D], tw48[:, 1, e:e + 1], None, ALU.mult).then_inc(ys_ok, 1)
            for e in range(NE):
                dve.wait_ge(es_ok, e + 1)
                at_least(dve, y_mm, e - 1)
                dve.tensor_tensor(ea[e % 2][:, :, :], EB[e % 3][0:IH, 2 * CAP:4 * CAP].rearrange("p (m q) -> p m q", m=2),
                                  es_[e % 2][:, :, :], ALU.mult).then_inc(ea_ok, 1)
                if e:
                    weighted(e - 1)
            weighted(NE - 1)

        @block.tensor
        def _(pe):
            pe.wait_ge(gw_in, 16)
            for c in range(DK):
                ins = pe.transpose(TB[0][:, c * NE:c * NE + NE], gw[:, c * P:c * P + P], identf[0:NE, 0:NE])
            ins.then_inc(gwT_mm, 1)
            pe.wait_ge(gwT_ok, 1)

            def logits(m):
                pe.wait_ge(hT_ok, m + 1)
                for c in range(DK):
                    ins = pe.matmul(LG[:, m * NE:m * NE + NE], hT[:, c, m * P:m * P + P], gwT[:, c, :], start=(c == 0), stop=(c == DK - 1))
                ins.then_inc(lg_mm, 1)
            for m in range(NB):
                pe.wait_ge(h_ok, m + 1)
                at_least(pe, hT_ok, m - 1)
                for c in range(DK):
                    ins = pe.transpose(TB[m % 2][:, c * P:c * P + P], h[m % 2][:, c * P:c * P + P], identf[:, :])
                ins.then_inc(hT_mm, 1)
                if m:
                    logits(m - 1)
            logits(NB - 1)
            pe.wait_ge(w2_in, 48)

            def up(k, f):
                i, (a, n) = 3 * k + f, FC[f]
                at_least(pe, ac_ok, i - 1)
                for w in range(2):
                    for c in range(DK):
                        ins = pe.matmul(GU[2 * (i % 2) + w][0:n, :], WSG[:, c, w * SHARED + a:w * SHARED + a + n],
                                        hT[:, c, 512 * k:512 * k + 512], start=(c == 0), stop=(c == DK - 1))
                ins.then_inc(up_mm, 1)

            def down(m):
                k, j = m // 4, m % 4
                pe.wait_ge(ac_ok, 3 * k + 3)
                at_least(pe, ro_ok, m)
                for f in range(3):
                    n = FC[f][1]
                    ins = pe.matmul(DN[:, 0:D], ac[k % 2][0:n, f, j * P:j * P + P], WSD[0:n, f, :], start=(f == 0), stop=(f == 2))
                ins.then_inc(dn_mm, 1)

            def cumulate(c):
                at_least(pe, cum_ok, c - 1)
                for i in range(4 * c + 4):
                    a = max(i - 4 * c, 0) * P
                    rhs = tri[:, 0:512 - a] if i >= 4 * c else ones4[:, :]
                    ins = pe.matmul(TB[c % 2][:, a:512], chosen4[:, i, :, :], rhs, start=(i == 0), stop=(i == 4 * c + 3))
                ins.then_inc(cum_mm, 1)

            for f in range(3):
                up(0, f)
            up(1, 0)
            for m in range(4):
                down(m)
            up(1, 1)
            pe.wait_ge(chosen_ok, 1)
            for c in range(2):
                cumulate(c)
            up(1, 2)
            for c in range(2, 4):
                cumulate(c)
            up(2, 0)
            for m in range(4, 8):
                down(m)
            up(2, 1)
            up(2, 2)
            up(3, 0)
            for m in range(8, 12):
                down(m)
            up(3, 1)
            up(3, 2)
            for m in range(12, 16):
                down(m)
            for r in range(R):
                pe.wait_ge(xg_in[r], 16)
                at_least(pe, xb_ok, r - 1)
                for c in range(DK):
                    ins = pe.transpose(TB[r % 2][:, c * P:c * P + P], xg[:, r, c * P:c * P + P], identf[:, :])
                ins.then_inc(xb_mm, 1)
            pe.wait_ge(tw_ok, 1)
            for r in range(R):
                ins = pe.matmul(LG[0:CAP, 0:2 * NE], place[:, r, :], tw[:, r, :, :], start=(r == 0), stop=(r == R - 1))
            ins.then_inc(tw_mm, 1)
            pe.wait_ge(xb_ok, R)

            def expert_down(e):
                pe.wait_ge(ea_ok, e + 1)
                at_least(pe, ys_ok, e - 1)
                for m in range(2):
                    ins = pe.matmul(YB[e % 2][0:CAP, 0:D], ea[e % 2][:, m, :], ring.dn[:, e % HALF, m, :], start=(m == 0), stop=(m == 1))
                ins.then_inc(y_mm, 1)
            for e in range(NE):
                s = e % HALF
                if s % LOT == 0:
                    pe.wait_ge(ring.lot_in[s // LOT], ring.LOADS * (1 + e // HALF))
                at_least(pe, ea_ok, e - 2)
                for j in range(4):
                    a = (j // 2) * INNER + j % 2
                    for c in range(DK):
                        ins = pe.matmul(EB[e % 3][0:IH, j * CAP:j * CAP + CAP], ring.gu[:, s, c, a:a + INNER - 1:2],
                                        xbT[:, c, e, :], start=(c == 0), stop=(c == DK - 1))
                ins.then_inc(eup_mm, 1)
                if e:
                    expert_down(e - 1)
            expert_down(NE - 1)


_INS = ["x", "ctx_1024", "fside_BxSx2_0", "L0_xattn_Wq", "L0_xattn_Wkv", "L0_xattn_Wout", "L0_xattn_bout",
        "L0_ffn_gate_w", "L0_ffn_w_gate_up", "L0_ffn_w_down", "L0_ffn_ws_gate_up", "L0_ffn_ws_down"]


def kernel(**inputs):
    import concourse.bacc as bacc
    from concourse.bass_utils import run_bass_kernel_spmd

    nc = bacc.Bacc("TRN2", target_bir_lowering=False, num_devices=1)
    arrays, args = {}, []
    for name in _INS:
        a = np.ascontiguousarray(inputs[name])
        arrays[f"in_{name}"] = a
        args.append(nc.dram_tensor(f"in_{name}", a.shape, F32, kind="ExternalInput").ap())
    out = nc.dram_tensor("out", (T + CAP, D), F32, kind="ExternalOutput").ap()
    build(nc, *args, out)
    r = run_bass_kernel_spmd(nc, [arrays], core_ids=[0])
    return r.results[0]["out"][:T].reshape(NB, P, D)
```

```python
from contextlib import ExitStack

import numpy as np

import concourse.bass as bass
from concourse import mybir

ALU = mybir.AluOpType
ACT = mybir.ActivationFunctionType
AX = mybir.AxisListType
F32 = mybir.dt.float32
F16 = mybir.dt.float16
U32 = mybir.dt.uint32

P = 128
NB, D, DC = 16, 256, 128
NH, HD = 32, 8
QUADS, SLOT = NH // 4, 32
DK = D // P
MAXROW = 3 * HD
SCALE = float(1.0 / np.sqrt(np.float32(HD)))
EPS = 1e-5
TWO_PI = 6.283185
BIG = 12582912.0
NE, INNER, TOPK, CAP = 32, 176, 6, 48
GROUPS, TOPG = 8, 3
SHARED = 2 * INNER
ROUTE_SCALE = 16.0
RESIDENT, LOT = 20, 2
IH = INNER // 2
T = NB * P
NPAIR, LANE = NE // 2, 64
COUNT_ACT = 4


class Batch:

    def __init__(self, half, par):
        self.half, self.par = half + par // 2, par % 2
        self.n = 2 * self.half + self.par

    def __add__(self, k):
        return Batch(self.half, self.par + k) if k >= 0 or self.par + k >= 0 else Batch(self.half - 1, self.par + k + 2)


def at_least(eng, sem, count):
    if not isinstance(count, int) or count > 0:
        eng.wait_ge(sem, count)


def build(nc, x, ctx_in, pos, wq, wkv, wout, bout, gate_w, w_gu, w_dn, ws_gu, ws_dn, out):
    with ExitStack() as es:
        def keep(name, shape, dt=F32):
            return es.enter_context(nc.sbuf_tensor(name, shape, dt))

        def sem(name):
            return es.enter_context(nc.semaphore(name))

        X = keep("X", [P, NB, D])
        identf = keep("identf", [P, P])
        st2 = keep("st2", [P, NB, 6])
        ring = Ring(nc, keep, sem, w_gu, w_dn)
        attention(nc, sem, X, identf, st2, ring, x, ctx_in, pos, wq, wkv, wout, bout)
        mixture(nc, sem, X, identf, st2, ring, gate_w, ws_gu, ws_dn, out)


class Ring:

    def __init__(self, nc, keep, sem, w_gu, w_dn):
        self.gu = keep("ring_gu", [P, RESIDENT, DK, 2 * INNER])
        self.dn = keep("ring_dn", [IH, RESIDENT, 2, D])
        self.lot_in = [sem(f"lot_in{n}") for n in range(RESIDENT // LOT)]
        self.w_gu = w_gu.rearrange("e (c p) f -> p e c f", p=P)
        self.w_dn = w_dn.rearrange("e (p m) n -> p e m n", m=2)

    def load(self, eng, lot):
        e, place = lot * LOT, lot % len(self.lot_in)
        a = place * LOT
        for k in range(LOT):
            eng.dma_start(self.gu[:, a + k, :, :], self.w_gu[:, e + k]).then_inc(self.lot_in[place], 16)
        eng.dma_start(self.dn[:, a:a + LOT, :, :], self.w_dn[:, e:e + LOT]).then_inc(self.lot_in[place], 16)

    LOADS = 16 * (LOT + 1)


def attention(nc, sem, X, identf, st2, ring, x, ctx_in, pos, wq, wkv, wout, bout):
    with ExitStack() as es:
        def sb(name, shape, dt=F32):
            return es.enter_context(nc.sbuf_tensor(name, shape, dt))

        POS = sb("POS", [P, NB, 2])
        WQ = sb("WQ", [P, DK, D])
        WKV = sb("WKV", [P, 2 * D])
        WO = sb("WO", [P, DK, D])
        BO = sb("BO", [P, D])
        identh = sb("identh", [P, P], F16)
        CT = [sb(f"CT{i}", [P, DC]) for i in range(2)]
        xn = sb("xn", [P, D])
        xcT = [sb(f"xcT{i}", [P, 3, P]) for i in range(2)]
        t1 = sb("t1", [P, 2 * D])
        t2 = sb("t2", [P, 2 * D])
        rot = sb("rot", [P, 2 * D])
        tokst = [sb(f"tokst{i}", [P, 2, NH, SLOT], F16) for i in range(2)]
        qst = [sb(f"qst{i}", [P, QUADS, P], F16) for i in range(2)]
        kT = sb("kT", [P, QUADS, P], F16)
        kz = [sb(f"kz{i}", [P, 4, QUADS, P], F16) for i in range(2)]
        V = [sb(f"V{i}", [P, NH, SLOT]) for i in range(2)]
        mx = [sb(f"mx{i}", [P, 4, 2], F16) for i in range(2)]
        mxs = [sb(f"mxs{i}", [8, P], F16) for i in range(2)]
        pw = [sb(f"pw{i}", [P, 4 * P]) for i in range(2)]
        OT = [sb(f"OT{i}", [P, 4, P]) for i in range(2)]
        rec = sb("rec", [P, 2, NH // 2])
        attn = sb("attn", [P, D])
        attnT = sb("attnT", [P, DK, P])
        st1 = sb("st1", [P, NB, 6])
        mv1 = sb("mv1", [P, NB, 2])
        rs1 = sb("rs1", [P, NB, 1])
        nb1 = sb("nb1", [P, NB, 1])
        ang = sb("ang", [P, 2, NB, 2, 2])
        turns = sb("turns", [P, 2, NB, 2, 2])
        RC = sb("RC", [P, NB, 4, 2])
        RS = sb("RS", [P, NB, 4, 2])
        bank = [es.enter_context(nc.psum_tensor(f"bank{i}", [P, 512], F32)) for i in range(8)]
        SB, STB, OB, M0, M1 = bank[0:2], bank[2:4], bank[4:6], bank[6], bank[7]

        x_in = [sem(f"x_in{i}") for i in range(4)]
        pos_in, w_in, bo_in = sem("pos_in"), sem("w_in"), sem("bo_in")
        ctx_in_s = [sem(f"ctx_in{i}") for i in range(2)]
        consts, consts2 = sem("consts"), sem("consts2")
        stat1, mv1_ok, std1, rs1_ok = sem("stat1"), sem("mv1_ok"), sem("std1"), sem("rs1_ok")
        turn_s, sin_s, rope_tab = sem("turn_s"), sem("sin_s"), sem("rope_tab")
        xn_ok, x_biased = sem("xn_ok"), sem("x_biased")
        xcT_mm, xcT_ok = sem("xcT_mm"), sem("xcT_ok")
        qk_mm, rope_ok, rot_ok, hi_ok, tokst_ok = sem("qk_mm"), sem("rope_ok"), sem("rot_ok"), sem("hi_ok"), sem("tokst_ok")
        qstT_mm, kstT_mm, qst_ok, kT_ok = sem("qstT_mm"), sem("kstT_mm"), sem("qst_ok"), sem("kT_ok")
        kz_in = [sem(f"kz_in{i}") for i in range(2)]
        v_mm, v_ok = sem("v_mm"), sem("v_ok")
        s_mm, max_ok, mxT_mm, mxs_ok = sem("s_mm"), sem("max_ok"), sem("mxT_mm"), sem("mxs_ok")
        mr_in = [sem(f"mr_in{i}") for i in range(2)]
        st_mm, exp_ok, pv_mm, OT_ok = sem("st_mm"), sem("exp_ok"), sem("pv_mm"), sem("OT_ok")
        ob_mm, rec_ok, attn_ok = sem("ob_mm"), sem("rec_ok"), sem("attn_ok")
        attnT_mm, attnT_ok, wo_mm, x1_ok, st2_ok = (sem(n) for n in ("attnT_mm", "attnT_ok", "wo_mm", "x1_ok", "st2_ok"))

        xr = x.rearrange("b p d -> p b d")

        def periods(eng, period):
            for n in range(-3, 2):
                period(Batch(n // 2, n % 2))
            with eng.Fori(0, 5) as i:
                for u in range(2):
                    period(Batch(i, 2 + u))
            for n in range(12, NB + 1):
                period(Batch(n // 2, n % 2))

        def inside(b, lo=0, hi=NB - 1):
            return not isinstance(b.n, int) or lo <= b.n <= hi

        block = es.enter_context(nc.Block())

        @block.sync
        def _(sp):
            sp.dma_start(POS[:, :, :], pos.rearrange("b p a -> p b a")).then_inc(pos_in, 16)
            for c in range(4):
                sp.dma_start(X[:, 4 * c:4 * c + 4, :], xr[:, 4 * c:4 * c + 4, :]).then_inc(x_in[c], 16)
                if c == 0:
                    sp.dma_start(CT[0][:, :], ctx_in[0]).then_inc(ctx_in_s[0], 16)
                    sp.dma_start(WQ[:, :, :], wq.rearrange("(c p) n -> p c n", p=P)).then_inc(w_in, 16)
                    sp.dma_start(WKV[:, :], wkv).then_inc(w_in, 16)
                    sp.dma_start(WO[:, :, :], wout.rearrange("(c p) n -> p c n", p=P)).then_inc(w_in, 16)
                    sp.dma_start(BO[:, :], bout.rearrange("(a n) -> a n", a=1).broadcast_to([P, D])).then_inc(bo_in, 16)
            sp.wait_ge(consts, 8)

            def period(b):
                m1, m4 = b + 1, b + 4
                if inside(m1):
                    at_least(sp, v_ok, m1.n + 1)
                    for j in range(4):
                        sp.dma_start(kz[m1.par][32 * j:32 * j + 32, j, :, :],
                                     kT[32 * j:32 * j + 32, :, :]).then_inc(kz_in[m1.par], 16)
                for g in (1, 3, 5, 7):
                    who, half = (b, (g + 3) // 2) if g < 5 else (m1, (g - 5) // 2)
                    if inside(who):
                        k = 4 * who.n + half
                        sp.wait_ge(mxs_ok, k + 1)
                        sp.dma_start(qst[who.par][MAXROW:P:SLOT, 2 * half:2 * half + 2, :],
                                     mxs[half % 2][:, :]).then_inc(mr_in[half % 2], 16)
                    if g == 1 and inside(m4):
                        at_least(sp, xcT_mm, m4.n - 1)
                        sp.wait_ge(consts, 8)
                        sp.dma_start(CT[m4.par][:, :], ctx_in[m4.n]).then_inc(ctx_in_s[m4.par], 16)
            periods(sp, period)

        @block.gpsimd
        def _(pool):
            pool.memset(identf[:, :], 0.0).then_inc(consts, 1)
            pool.memset(identh[:, :], 0.0).then_inc(consts, 1)
            for i in range(2):
                pool.memset(kz[i][:, :, :, :], 0.0).then_inc(consts, 1)
                pool.memset(V[i][:, :, HD + 1:SLOT], 0.0).then_inc(consts, 1)
                pool.memset(V[i][:, :, HD:HD + 1], 1.0).then_inc(consts, 1)
            pool.wait_ge(consts, 2)
            for m in (identf, identh):
                pool.affine_select(out=m[:, :], in_=m[:, :], compare_op=ALU.not_equal, fill=1.0, base=0,
                                   pattern=[[-1, P]], channel_multiplier=1).then_inc(consts2, 1)
            for i in range(2):
                pool.memset(tokst[i][:, :, :, MAXROW:SLOT], 0.0).then_inc(consts2, 1)
            pool.wait_ge(consts2, 4)
            for i in range(2):
                pool.memset(tokst[i][:, 1, :, MAXROW:MAXROW + 1], 1.0).then_inc(consts2, 1)

            def split(m):
                at_least(pool, rope_ok, m.n + 1)
                at_least(pool, tokst_ok, 2 * m.n)
                pool.tensor_tensor(rot[:, :], t1[:, :], t2[:, :], ALU.add).then_inc(rot_ok, 1)
                pool.wait_ge(consts2, 6)
                at_least(pool, rot_ok, m.n + 1)
                ts = tokst[m.par]
                r4 = rot[:, :].rearrange("p (w h d) -> p w h d", w=2, d=HD)
                pool.tensor_copy(ts[:, :, :, 0:HD], r4).then_inc(hi_ok, 1)
                pool.wait_ge(consts2, 6)
                at_least(pool, hi_ok, m.n + 1)
                hi = ts[:, :, :, 0:HD]
                for w in range(2):
                    a = (2 - w) * HD
                    pool.tensor_tensor(ts[:, w, :, a:a + HD], r4[:, w], hi[:, w], ALU.subtract)
                    a = (1 + w) * HD
                    pool.tensor_copy(ts[:, w, :, a:a + HD], hi[:, w]).then_inc(tokst_ok, 1)

            def add_bias(m):
                at_least(pool, xn_ok, m.n + 1)
                pool.tensor_tensor(X[:, m.n, :], X[:, m.n, :], BO[:, :], ALU.add).then_inc(x_biased, 1)

            pool.wait_ge(bo_in, 16)

            def period(b):
                if inside(b + 3):
                    add_bias(b + 3)
                    split(b + 3)
            periods(pool, period)

        @block.scalar
        def _(act):
            for lot in range(RESIDENT // LOT):
                ring.load(act, lot)
            act.wait_ge(turn_s, 5)
            act.activation(ang[:, :, :, :, :], turns[:, :, :, :, :], ACT.Sin, scale=TWO_PI).then_inc(sin_s, 1)
            act.wait_ge(mv1_ok, 2)
            act.activation(rs1[:, :, 0], nb1[:, :, 0], ACT.Sqrt).then_inc(std1, 1)

            def norm(m):
                act.wait_ge(rs1_ok, 2)
                at_least(act, xcT_mm, m.n)
                act.activation(xn[:, :], X[:, m.n, :], ACT.Identity, bias=nb1[:, m.n, :],
                               scale=rs1[:, m.n, :]).then_inc(xn_ok, 1)

            def evac_xcT(m):
                at_least(act, xcT_mm, m.n + 1)
                at_least(act, v_mm, m.n - 1)
                act.copy(xcT[m.par][:, :, :], M1[:, 0:3 * P].rearrange("p (c t) -> p c t", c=3)).then_inc(xcT_ok, 1)

            norm(Batch(0, 0))

            def period(b):
                m1, m2, m3, m4, o = b + 1, b + 2, b + 3, b + 4, b + -1
                for g in range(QUADS):
                    if inside(b):
                        act.wait_ge(st_mm, QUADS * b.n + g + 1)
                        at_least(act, pv_mm, QUADS * b.n + g - 1)
                        act.activation(pw[g % 2][:, :], STB[g % 2][:, :], ACT.Exp, scale=SCALE).then_inc(exp_ok, 1)
                    if g == 0 and inside(m1):
                        at_least(act, v_mm, m1.n + 1)
                        at_least(act, pv_mm, QUADS * b.n)
                        act.copy(V[m1.par][:, :, 0:HD], M0[:, 0:D].rearrange("p (h d) -> p h d", d=HD)).then_inc(v_ok, 1)
                    if g == 0 and inside(m3):
                        evac_xcT(m3)
                    if g == 1 and inside(m1):
                            at_least(act, qstT_mm, m1.n + 1)
                            at_least(act, st_mm, QUADS * b.n)
                            act.copy(qst[m1.par][:, :, :], M0[:, :].bitcast(F16).rearrange("p (q t) -> p q t", q=QUADS)).then_inc(qst_ok, 1)
                    if g == 2 and inside(o):
                        evac_OT(o, 1)
                    if g == 3 and inside(m4):
                        norm(m4)
                    if g == 5 and inside(b):
                        evac_OT(b, 0)
                    if g == 5 and inside(o):
                        act.wait_ge(attnT_mm, o.n + 1)
                        at_least(act, wo_mm, o.n)
                        act.copy(attnT[:, :, :], M0[:, D:2 * D].rearrange("p (c t) -> p c t", c=DK)).then_inc(attnT_ok, 1)
                    if g == 6 and inside(m2):
                        at_least(act, kstT_mm, m2.n + 1)
                        if inside(m1):
                            act.wait_ge(kz_in[m1.par], 64 * (m1.half + 1))
                        act.copy(kT[:, :, :], M1[:, :].bitcast(F16).rearrange("p (q t) -> p q t", q=QUADS)).then_inc(kT_ok, 1)

            def evac_OT(m, half):
                act.wait_ge(pv_mm, QUADS * m.n + 4 * half + 4)
                at_least(act, ob_mm, 2 * m.n + half - 1)
                act.copy(OT[half][:, :, :], OB[half][:, :].rearrange("p (q t) -> p q t", q=4)).then_inc(OT_ok, 1)
            periods(act, period)

        @block.vector
        def _(dve):
            freq = [float(np.float32(10000.0) ** np.float32(-f / 2)) for f in range(2)]
            dve.wait_ge(pos_in, 16)
            for f in range(2):
                for c in range(2):
                    dve.tensor_scalar(turns[:, c, :, :, f], POS[:, :, :], freq[f] / (2 * np.pi), 0.25 * c,
                                      ALU.mult, ALU.add).then_inc(turn_s, 1)
            dve.wait_ge(turn_s, 4)
            dve.tensor_scalar(ang[:, :, :, :, :], turns[:, :, :, :, :], BIG, BIG, ALU.add, ALU.subtract).then_inc(rope_tab, 1)
            dve.wait_ge(rope_tab, 1)
            dve.tensor_tensor(turns[:, :, :, :, :], turns[:, :, :, :, :], ang[:, :, :, :, :], ALU.subtract).then_inc(turn_s, 1)
            for c in range(4):
                dve.wait_ge(x_in[c], 16)
                for j in range(4 * c, 4 * c + 4):
                    dve.bn_stats(st1[:, j, :], X[:, j, :]).then_inc(stat1, 1)
            for j in range(NB):
                dve.wait_ge(stat1, j + 1)
                ins = dve.bn_aggr(mv1[:, j, :], st1[:, j, :])
            ins.then_inc(mv1_ok, 1)
            dve.wait_ge(mv1_ok, 1)
            dve.tensor_scalar(nb1[:, :, 0], mv1[:, :, 1], EPS, None, ALU.add).then_inc(mv1_ok, 1)
            dve.wait_ge(sin_s, 1)
            sin = ang[:, 0].rearrange("p b a f -> p b (a f)")
            cos = ang[:, 1].rearrange("p b a f -> p b (a f)")
            for r in range(2):
                dve.tensor_copy(RC[:, :, :, r], cos)
                dve.tensor_scalar(RS[:, :, :, r], sin, -1.0 if r == 0 else 1.0, None, ALU.mult).then_inc(rope_tab, 1)
            dve.wait_ge(std1, 1)
            dve.reciprocal(rs1[:, :, 0], rs1[:, :, 0]).then_inc(rs1_ok, 1)
            dve.wait_ge(rs1_ok, 1)
            dve.scalar_tensor_tensor(out=nb1[:, :, 0], in0=mv1[:, :, 0], scalar=-1.0, in1=rs1[:, :, 0],
                                     op0=ALU.mult, op1=ALU.mult).then_inc(rs1_ok, 1)
            dve.wait_ge(rope_tab, 3)

            def rope(m):
                at_least(dve, qk_mm, m.n + 1)
                at_least(dve, rot_ok, m.n)
                qk = M1[:, :].rearrange("p (x a r) -> p x a r", a=4, r=2)
                o1 = t1[:, :].rearrange("p (x a) -> p x a", a=8)
                o2 = t2[:, :].rearrange("p (x a r) -> p x a r", a=4, r=2)
                rc = RC[:, m.n].rearrange("p a r -> p (a r)").unsqueeze(1).broadcast_to([P, 2 * NH, 8])
                dve.tensor_tensor(o1, M1[:, :].rearrange("p (x a) -> p x a", a=8), rc, ALU.mult)
                for r in range(2):
                    rs = RS[:, m.n, :, r].unsqueeze(1).broadcast_to([P, 2 * NH, 4])
                    ins = dve.tensor_tensor(o2[:, :, :, r], qk[:, :, :, 1 - r], rs, ALU.mult)
                ins.then_inc(rope_ok, 1)

            def row_max(m, u):
                dve.wait_ge(s_mm, QUADS * m.n + u + 1)
                if not (isinstance(m.n, int) and 4 * m.n + u // 2 < 2):
                    dve.wait_ge(mxT_mm, 4 * m.n + u // 2 - 1)
                dve.tensor_reduce(mx[u // 2 % 2][:, :, u % 2], SB[u % 2][:, :].rearrange("p (j t) -> p j t", j=4),
                                  axis=AX.X, op=ALU.max, negate=True).then_inc(max_ok, 1)

            def evac_max(m, half):
                k = 4 * m.n + half
                dve.wait_ge(mxT_mm, k + 1)
                at_least(dve, mr_in[half % 2], 16 * (2 * m.n + half // 2))
                dve.tensor_copy(mxs[half % 2][:, :], SB[1][0:8, 0:P // 2].bitcast(F16)).then_inc(mxs_ok, 1)

            def normalise(m, half):
                at_least(dve, ob_mm, 2 * m.n + half + 1)
                ob = OB[half][:, :].rearrange("p (h s) -> p h s", s=SLOT)
                at_least(dve, attn_ok, 2 * m.n + half)
                dve.reciprocal(rec[:, half, :], ob[:, :, HD]).then_inc(rec_ok, 1)
                at_least(dve, attnT_mm, m.n)
                dve.wait_ge(rec_ok, 2 * m.n + half + 1)
                dve.tensor_tensor(attn[:, half * P:half * P + P].rearrange("p (h d) -> p h d", d=HD), ob[:, :, 0:HD],
                                  rec[:, half, :].unsqueeze(2).broadcast_to([P, NH // 2, HD]), ALU.mult).then_inc(attn_ok, 1)

            def period(b):
                m1, m3, o = b + 1, b + 3, b + -1
                for g in range(QUADS):
                    who, u = (b, g + 5) if g < 3 else (m1, g - 3)
                    if inside(who):
                        row_max(who, u)
                    if g % 2 == 1:
                        who, half = (b, (g + 3) // 2) if g < 5 else (m1, (g - 5) // 2)
                        if inside(who):
                            evac_max(who, half)
                    if g == 0 and inside(o):
                        normalise(o, 0)
                    if g == 3 and inside(o):
                        normalise(o, 1)
                    if g == 3 and inside(m3):
                        rope(m3)
                    if g == 7 and inside(o):
                        dve.wait_ge(wo_mm, o.n + 1)
                        dve.wait_ge(x_biased, o.n + 1)
                        dve.tensor_tensor(X[:, o.n, :], M0[:, 0:D], X[:, o.n, :], ALU.add).then_inc(x1_ok, 1)
                        dve.wait_ge(x1_ok, o.n + 1)
                        dve.wait_ge(rope_tab, 3)
                        dve.bn_stats(st2[:, o.n, :], X[:, o.n, :]).then_inc(st2_ok, 1)
            periods(dve, period)

        @block.tensor
        def _(pe):
            pe.wait_ge(consts2, 6)
            pe.wait_ge(consts, 8)

            def transpose_xc(m):
                at_least(pe, xn_ok, m.n + 1)
                pe.wait_ge(ctx_in_s[m.par], 16 * (m.half + 1))
                at_least(pe, rope_ok, m.n)
                at_least(pe, kT_ok, m.n - 1)
                for c in range(DK):
                    pe.transpose(M1[:, c * P:c * P + P], xn[:, c * P:c * P + P], identf[:, :])
                pe.transpose(M1[:, DK * P:DK * P + P], CT[m.par][:, :], identf[:, :]).then_inc(xcT_mm, 1)

            def project_qk(m):
                at_least(pe, xcT_ok, m.n + 1)
                for c in range(DK):
                    pe.matmul(M1[:, 0:D], xcT[m.par][:, c, :], WQ[:, c, :], start=(c == 0), stop=(c == DK - 1))
                pe.matmul(M1[:, D:2 * D], xcT[m.par][:, DK, :], WKV[:, 0:D], start=True, stop=True).then_inc(qk_mm, 1)

            def transpose_q(m):
                at_least(pe, v_ok, m.n + 1)
                for q in range(QUADS):
                    ins = pe.transpose(M0[:, q * 64:q * 64 + 64].bitcast(F16), tokst[m.par][:, 0, 4 * q:4 * q + 4, :], identh[:, :])
                ins.then_inc(qstT_mm, 1)

            def transpose_k(m):
                at_least(pe, tokst_ok, 2 * m.n + 2)
                at_least(pe, rope_ok, min(m.n + 2, NB) if isinstance(m.n, int) else m.n + 2)
                for q in range(QUADS):
                    ins = pe.transpose(M1[:, q * 64:q * 64 + 64].bitcast(F16), tokst[m.par][:, 1, 4 * q:4 * q + 4, :], identh[:, :])
                ins.then_inc(kstT_mm, 1)

            def project_v(m):
                at_least(pe, x1_ok, m.n - 2)
                pe.matmul(M0[:, 0:D], xcT[m.par][:, DK, :], WKV[:, D:2 * D], start=True, stop=True).then_inc(v_mm, 1)

            def logits_q(m, u):
                if u == 0:
                    at_least(pe, qst_ok, m.n + 1)
                    pe.wait_ge(kz_in[m.par], 64 * (m.half + 1))
                at_least(pe, max_ok, QUADS * m.n + u - 1)
                if u % 2:
                    at_least(pe, mxs_ok, 4 * m.n + u // 2)
                pe.matmul(SB[u % 2][:, :], qst[m.par][:, u, :], kz[m.par][:, :, u, :], start=True, stop=True).then_inc(s_mm, 1)

            def transpose_max(m, half):
                pe.wait_ge(max_ok, QUADS * m.n + 2 * half + 2)
                pe.transpose(SB[1][0:8, 0:P // 2].bitcast(F16), mx[half % 2][:, :, :], identh[:, :]).then_inc(mxT_mm, 1)

            def logits_k(m, g):
                at_least(pe, exp_ok, QUADS * m.n + g - 1)
                if g % 2 == 0:
                    half = g // 2
                    pe.wait_ge(mr_in[half % 2], 16 * (2 * m.n + half // 2 + 1))
                for j in range(4):
                    ins = pe.matmul(STB[g % 2][:, j * P:j * P + P], kz[m.par][:, j, g, :], qst[m.par][:, g, :],
                                    start=True, stop=True)
                ins.then_inc(st_mm, 1)

            def weigh_values(m, g):
                pe.wait_ge(exp_ok, QUADS * m.n + g + 1)
                if g == 0:
                    at_least(pe, v_ok, m.n + 1)
                if g % 4 == 0:
                    at_least(pe, attn_ok, 2 * m.n + g // 4 - 1)
                for j in range(4):
                    ins = pe.matmul(OB[g // 4][32 * j:32 * j + 32, (g % 4) * P:(g % 4) * P + P], V[m.par][:, 4 * g + j, :],
                                    pw[g % 2][:, j * P:j * P + P], start=True, stop=True, tile_position=(0, 32 * j))
                ins.then_inc(pv_mm, 1)

            def transpose_outputs(m, half):
                pe.wait_ge(OT_ok, 2 * m.n + half + 1)
                for q in range(4):
                    ins = pe.transpose(OB[half][:, q * P:q * P + P], OT[half][:, q, :], identf[:, :])
                ins.then_inc(ob_mm, 1)

            def transpose_attn(m):
                pe.wait_ge(attn_ok, 2 * m.n + 2)
                pe.wait_ge(qst_ok, min(m.n + 3, NB) if isinstance(m.n, int) else m.n + 3)
                for c in range(DK):
                    ins = pe.transpose(M0[:, D + c * P:D + c * P + P], attn[:, c * P:c * P + P], identf[:, :])
                ins.then_inc(attnT_mm, 1)

            def project_out(m):
                pe.wait_ge(attnT_ok, m.n + 1)
                for c in range(DK):
                    ins = pe.matmul(M0[:, 0:D], attnT[:, c, :], WO[:, c, :], start=(c == 0), stop=(c == DK - 1))
                ins.then_inc(wo_mm, 1)

            pe.wait_ge(w_in, 48)

            def period(b):
                m1, m2, m3, o = b + 1, b + 2, b + 3, b + -1
                for g in range(QUADS):
                    if inside(b):
                        logits_k(b, g)
                    who, u = (b, g + 5) if g < 3 else (m1, g - 3)
                    if inside(who):
                        logits_q(who, u)
                    if g == 0 and inside(m1):
                        project_v(m1)
                    if g == 0 and inside(o):
                        weigh_values(o, QUADS - 1)
                    if g > 0 and inside(b):
                        weigh_values(b, g - 1)
                    if g == 0 and inside(m3):
                        transpose_xc(m3)
                    if g == 1 and inside(m1):
                        transpose_q(m1)
                    if g == 2:
                        if inside(m3):
                            project_qk(m3)
                    if g == 3 and inside(o):
                        transpose_outputs(o, 1)
                    if g == 4 and inside(o):
                        transpose_attn(o)
                    if g == 5 and inside(m2):
                        transpose_k(m2)
                    if g == 6 and inside(o):
                        project_out(o)
                    if g == 7 and inside(b):
                        transpose_outputs(b, 0)
                    if g % 2 == 1:
                        who, half = (b, (g + 3) // 2) if g < 5 else (m1, (g - 5) // 2)
                        if inside(who):
                            transpose_max(who, half)
            periods(pe, period)


def mixture(nc, sem, X, identf, st2, ring, gate_w, ws_gu, ws_dn, out):
    G4, R = 4, CAP // 4
    FC = [(0, 128), (128, 128), (256, SHARED - 256)]
    ROW = D + NE
    with ExitStack() as es:
        def sb(name, shape, dt=F32):
            return es.enter_context(nc.sbuf_tensor(name, shape, dt))

        table = nc.dram_tensor("table", (T, ROW), F32, kind="Internal").ap()
        odd = nc.dram_tensor("odd", (T + CAP, D), F32, kind="Internal").ap()
        hT = sb("hT", [P, DK, T])
        h = [sb(f"h{i}", [P, D]) for i in range(2)]
        mv2 = sb("mv2", [P, NB, 2])
        rs2 = sb("rs2", [P, NB])
        nb2 = sb("nb2", [P, NB])
        gw = sb("gw", [NE, D])
        gwT = sb("gwT", [P, DK, NE])
        WSG = sb("WSG", [P, DK, 2 * SHARED])
        WSD = sb("WSD", [P, 3, D])
        zero = sb("zero", [P, D])
        gv = sb("gv", [P, NB, 8])
        gi = sb("gi", [P, NB, 8], U32)
        io8 = sb("io8", [P, GROUPS])
        ex = sb("ex", [P, NB, NE])
        wt = sb("wt", [P, NB, NE])
        smx = sb("smx", [P, NB])
        ssum = sb("ssum", [P, NB])
        eih = sb("eih", [P, NB, 8], F16)
        io32 = sb("io32", [P, NE], F16)
        chosen = sb("chosen", [P, NB, NE], F16)
        tri = sb("tri", [P, 4 * P], F16)
        ones4 = sb("ones4", [P, 4 * P], F16)
        cum = sb("cum", [P, T], F16)
        thr = sb("thr", [P, R])
        thr_half = sb("thr_half", [P, R])
        tok = sb("tok", [P, R])
        toki = sb("toki", [P, R], U32)
        own = sb("own", [P, NE])
        io64 = sb("io64", [P, 2 * LANE])
        place = sb("place", [P, R, 2 * LANE])
        tw = sb("tw", [P, R, 2, NE])
        xg = sb("xg", [P, R, ROW])
        xgf = xg[:, :, :].rearrange("p r d -> p (r d)")
        junk, junk2 = (xgf[:, i * T // 2:(i + 1) * T // 2].bitcast(F16) for i in range(2))
        chosen4 = xgf[:, T:T + NB * G4 * NE // 2].bitcast(F16).rearrange("p (b g e) -> p b g e", b=NB, g=G4)
        xbT = sb("xbT", [P, DK, NE * CAP + LANE - CAP])
        sc = xbT[:, 0, 0:NB * NE].rearrange("p (b e) -> p b e", b=NB)
        eq = [xbT[:, 0, (2 + i) * NB * NE // 2:(3 + i) * NB * NE // 2].bitcast(F16).rearrange("p (b e) -> p b e", b=NB) for i in range(2)]
        gm, gif, *kp = (xbT[:, 1, i * NB * 8:(i + 1) * NB * 8].rearrange("p (b g) -> p b g", b=NB) for i in range(2 + TOPG))
        pcol = sb("pcol", [CAP, 1])
        twp = sb("twp", [P, 2, NE])
        wpair = sb("wpair", [P, NPAIR])
        inv = sb("inv", [CAP, NE])
        dst = sb("dst", [CAP, NE], U32)
        sg = [sb(f"sg{i}", [P, 512]) for i in range(2)]
        ac = [sb(f"ac{i}", [P, 3, 512]) for i in range(2)]
        ro = [sb(f"ro{i}", [P, D]) for i in range(2)]
        acf = [ac[i][:, :, :].rearrange("p f t -> p (f t)") for i in range(2)]
        es_ = [acf[i][:, 0:INNER].rearrange("p (m q) -> p m q", m=2) for i in range(2)]
        ea = [acf[i][:, INNER:2 * INNER].rearrange("p (m q) -> p m q", m=2) for i in range(2)]
        eaT = [acf[i][0:IH, 2 * INNER:2 * INNER + 2 * P].rearrange("p (m q) -> p m q", m=2) for i in range(2)]
        ys = [acf[i // 2][:, 640 + D * (i % 2):640 + D * (i % 2) + D] for i in range(3)]
        bank = [es.enter_context(nc.psum_tensor(f"mbank{i}", [P, 512], F32)) for i in range(8)]
        GU, DN, TB, LG = bank[0:4], bank[4], bank[5:7], bank[7]
        EB, YB, ET = bank[0:3], bank[3:5], bank[5:7]

        w2_in, gw_in, zero_ok, zero_in = sem("w2_in"), sem("gw_in"), sem("zero_ok"), sem("zero_in")
        mc_ok, mc2_ok = sem("mc_ok"), sem("mc2_ok")
        mv2_ok, std2, rs2_ok = sem("mv2_ok"), sem("std2"), sem("rs2_ok")
        h_ok, h_in, hT_mm, hT_ok = sem("h_ok"), [sem(f"h_in{i}") for i in range(2)], sem("hT_mm"), sem("hT_ok")
        gwT_mm, gwT_ok, lg_mm = sem("gwT_mm"), sem("gwT_ok"), sem("lg_mm")
        route, sc_ok, ex_ok, wt_ok, wt_in = sem("route"), sem("sc_ok"), sem("ex_ok"), sem("wt_ok"), sem("wt_in")
        chosen_ok, cum_mm, cum_ok = sem("chosen_ok"), sem("cum_mm"), sem("cum_ok")
        cnt_act, cnt_ok, toki_ok, xg_in = sem("cnt_act"), sem("cnt_ok"), sem("toki_ok"), [sem(f"xg_in{r}") for r in range(R)]
        tw_ok, tw_mm, tw48_ok, dst_ok = sem("tw_ok"), sem("tw_mm"), sem("tw48_ok"), sem("dst_ok")
        xb_mm, xb_ok = sem("xb_mm"), sem("xb_ok")
        up_mm, sg_ok, ac_ok, dn_mm, ro_ok = sem("up_mm"), sem("sg_ok"), sem("ac_ok"), sem("dn_mm"), sem("ro_ok")
        ro_in = [sem(f"ro_in{i}") for i in range(2)]
        eup_mm, es_ok, ea_ok, eaT_mm, eaT_ok, y_mm, ys_ok = (sem(n) for n in ("eup_mm", "es_ok", "ea_ok", "eaT_mm", "eaT_ok", "y_mm", "ys_ok"))
        sum_in = sem("sum_in")
        add_in = [sem("add_in_even"), sem("add_in_odd")]

        block = es.enter_context(nc.Block())

        @block.sync
        def _(sp):
            sp.dma_start(gw[:, :], gate_w).then_inc(gw_in, 16)
            sp.dma_start(WSG[:, :, :], ws_gu.rearrange("(c p) f -> p c f", p=P)).then_inc(w2_in, 16)
            sp.dma_start(WSD[:, 0:2, :], ws_dn[0:256].rearrange("(c p) n -> p c n", p=P)).then_inc(w2_in, 16)
            sp.dma_start(WSD[0:FC[2][1], 2, :], ws_dn[256:SHARED]).then_inc(w2_in, 16)
            sp.wait_ge(zero_ok, 1)
            sp.dma_start(out[T:T + CAP, :], zero[0:CAP, :]).then_inc(zero_in, 16)
            sp.dma_start(odd[0:T, :].rearrange("(b p) d -> p b d", p=P), zero[:, :].unsqueeze(1).broadcast_to([P, NB, D])).then_inc(zero_in, 16)
            sp.dma_start(odd[T:T + CAP, :], zero[0:CAP, :]).then_inc(zero_in, 16)
            for m in range(NB):
                sp.wait_ge(h_ok, m + 1)
                sp.dma_start(table[m * P:m * P + P, 0:D], h[m % 2][:, :]).then_inc(h_in[m % 2], 16)
            for m in range(NB):
                if m == 4:
                    sp.wait_ge(wt_ok, 1)
                    sp.dma_start(table[:, D:ROW].rearrange("(b p) e -> p b e", p=P), wt[:, :, :]).then_inc(wt_in, 16)
                sp.wait_ge(ro_ok, m + 1)
                sp.dma_start(out[m * P:m * P + P, :], ro[m % 2][:, :]).then_inc(ro_in[m % 2], 16)
            for lot in range(RESIDENT // LOT, NE // LOT):
                sp.wait_ge(y_mm, LOT // 2 * (lot + 1 - RESIDENT // LOT))
                ring.load(sp, lot)

        @block.gpsimd
        def _(pool):
            pool.memset(zero[:, :], 0.0).then_inc(zero_ok, 1)
            pool.memset(tri[:, :], 1.0).then_inc(mc_ok, 1)
            pool.memset(ones4[:, :], 1.0).then_inc(mc2_ok, 1)
            pool.wait_ge(mc_ok, 1)
            pool.affine_select(out=tri[:, 0:P], in_=tri[:, 0:P], compare_op=ALU.is_ge, fill=0.0, base=0,
                               pattern=[[1, P]], channel_multiplier=-1).then_inc(mc2_ok, 1)
            pool.iota(io8[:, :], [[1, GROUPS]], base=0, channel_multiplier=0, allow_small_or_imprecise_dtypes=True).then_inc(mc2_ok, 1)
            pool.iota(io32[:, :], [[1, NE]], base=0, channel_multiplier=0, allow_small_or_imprecise_dtypes=True).then_inc(mc2_ok, 1)
            pool.iota(io64[:, :], [[0, 2], [1, LANE]], base=0, channel_multiplier=0, allow_small_or_imprecise_dtypes=True).then_inc(mc2_ok, 1)
            pool.memset(xbT[:, :, NE * CAP:], 0.0).then_inc(mc2_ok, 1)
            pool.iota(pcol[:, :], [[0, 1]], base=0, channel_multiplier=1, allow_small_or_imprecise_dtypes=True).then_inc(mc2_ok, 1)
            for g in range(G4):
                rows = slice(NE * g, NE * g + NE)
                pool.wait_ge(mc2_ok, 7 + 2 * g)
                pool.iota(thr[rows, :], [[1, R]], base=R * g, channel_multiplier=0, allow_small_or_imprecise_dtypes=True).then_inc(mc2_ok, 1)
                pool.iota(own[rows, :], [[1, NE]], base=0, channel_multiplier=-1, allow_small_or_imprecise_dtypes=True).then_inc(mc2_ok, 1)
            for r in range(R):
                if r == 0:
                    pool.wait_ge(toki_ok, 1)
                    for i in range(2):
                        pool.wait_ge(h_in[i], 16 * (NB // 2))
                    pool.wait_ge(wt_in, 16)
                pool.indirect_dma_start(xg[:, r, :], None, table[:, :], bass.IndirectOffsetOnAxis(ap=toki[:, r:r + 1], axis=0)
                                        ).then_inc(xg_in[r], 16)
            pool.wait_ge(zero_in, 48)
            for i in range(2):
                pool.wait_ge(ro_in[i], 16 * (NB // 2))

            for k in range(NPAIR):
                for w, to in ((0, out), (1, odd)):
                    rows = slice(LANE * w, LANE * w + CAP)
                    pool.wait_ge(ys_ok, k + 1)
                    at_least(pool, add_in[w], 16 * k)
                    pool.indirect_dma_start(to[:, :], bass.IndirectOffsetOnAxis(ap=dst[:, 2 * k + w:2 * k + w + 1], axis=0),
                                            ys[k % 3][rows, :], None, compute_op=ALU.add).then_inc(add_in[w], 16)
            for w in range(2):
                pool.wait_ge(add_in[w], 16 * NPAIR)
            pool.dma_start(out[0:T, :], odd[0:T, :], accum_op=ALU.add, max_dma_last_dim=8192).then_inc(sum_in, 16)
            pool.wait_ge(sum_in, 16)

        @block.scalar
        def _(act):
            act.wait_ge(mv2_ok, 2)
            act.activation(rs2[:, :], nb2[:, :], ACT.Sqrt).then_inc(std2, 1)
            act.wait_ge(gwT_mm, 1)
            act.copy(gwT[:, :, :], TB[0][:, 0:DK * NE].rearrange("p (c e) -> p c e", c=DK)).then_inc(gwT_ok, 1)
            act.wait_ge(rs2_ok, 2)
            for m in range(NB):
                at_least(act, hT_mm, m - 1)
                at_least(act, h_in[m % 2], 16 * (m // 2))
                act.activation(h[m % 2][:, :], X[:, m, :], ACT.Identity, bias=nb2[:, m:m + 1],
                               scale=rs2[:, m:m + 1]).then_inc(h_ok, 1)

            def gate(k, f):
                c, n = 3 * k + f, FC[f][1]
                act.wait_ge(up_mm, c + 1)
                at_least(act, ac_ok, c - 1)
                act.activation(sg[c % 2][0:n, :], GU[2 * (c % 2)][0:n, :], ACT.Silu).then_inc(sg_ok, 1)
            for f in range(3):
                gate(0, f)
            act.wait_ge(sc_ok, 1)
            act.activation(ex[:, :, :], sc[:, :, :], ACT.Exp).then_inc(ex_ok, 1)
            for k in range(1, 4):
                for f in range(3):
                    gate(k, f)
                if k == 2:
                    act.wait_ge(cum_ok, 4)
                    act.wait_ge(cnt_ok, 1)
                    for r in range(R - COUNT_ACT, R):
                        if r > R - COUNT_ACT:
                            act.wait_ge(cnt_act, r - (R - COUNT_ACT))
                        act.activation(junk2, cum[:, :], ACT.Sign, bias=thr_half[:, r:r + 1], scale=-1.0,
                                       accum_out=tok[:, r:r + 1]).then_inc(cnt_act, 1)
            for r in range(R):
                act.wait_ge(xb_mm, r + 1)
                for c in range(DK):
                    ins = act.copy(xbT[:, c, 0:NE * CAP].rearrange("p (e g r) -> p r g e", e=NE, g=G4)[:, r],
                                   TB[r % 2][:, c * P:c * P + P].rearrange("p (g e) -> p g e", g=G4))
                ins.then_inc(xb_ok, 1)

            def evac_eaT(k):
                act.wait_ge(eaT_mm, k + 1)
                at_least(act, y_mm, k - 1)
                act.copy(eaT[k % 2][:, :, :], ET[k % 2][0:IH, 0:2 * P].rearrange("p (m q) -> p m q", m=2)).then_inc(eaT_ok, 1)
            for k in range(NPAIR):
                act.wait_ge(eup_mm, k + 1)
                at_least(act, ea_ok, k - 1)
                act.activation(es_[k % 2][:, :, :], EB[k % 3][:, 0:INNER].rearrange("p (q m) -> p m q", m=2), ACT.Silu).then_inc(es_ok, 1)
                if k:
                    evac_eaT(k - 1)
            evac_eaT(NPAIR - 1)

        @block.vector
        def _(dve):
            done = [0]

            def step(ins):
                done[0] += 1
                ins.then_inc(route, 1)
                dve.wait_ge(route, done[0])

            for m in range(NB):
                ins = dve.bn_aggr(mv2[:, m, :], st2[:, m, :])
            ins.then_inc(mv2_ok, 1)
            dve.wait_ge(mv2_ok, 1)
            dve.tensor_scalar(nb2[:, :], mv2[:, :, 1], EPS, None, ALU.add).then_inc(mv2_ok, 1)
            dve.wait_ge(std2, 1)
            dve.reciprocal(rs2[:, :], rs2[:, :]).then_inc(rs2_ok, 1)
            dve.wait_ge(rs2_ok, 1)
            dve.scalar_tensor_tensor(out=nb2[:, :], in0=mv2[:, :, 0], scalar=-1.0, in1=rs2[:, :],
                                     op0=ALU.mult, op1=ALU.mult).then_inc(rs2_ok, 1)
            for m in range(NB):
                dve.wait_ge(hT_mm, m + 1)
                dve.tensor_copy(hT[:, :, m * P:m * P + P], TB[m % 2][:, 0:D].rearrange("p (c t) -> p c t", c=DK)).then_inc(hT_ok, 1)

            def gated(k, f):
                c, n = 3 * k + f, FC[f][1]
                dve.wait_ge(sg_ok, c + 1)
                at_least(dve, dn_mm, 4 * (k - 1))
                dve.tensor_tensor(ac[k % 2][0:n, f, :], GU[2 * (c % 2) + 1][0:n, :], sg[c % 2][0:n, :], ALU.mult).then_inc(ac_ok, 1)

            def residual(m):
                dve.wait_ge(dn_mm, m + 1)
                at_least(dve, ro_in[m % 2], 16 * (m // 2))
                dve.tensor_tensor(ro[m % 2][:, :], DN[:, 0:D], X[:, m, :], ALU.add).then_inc(ro_ok, 1)

            dve.wait_ge(lg_mm, NB)
            dve.wait_ge(mc2_ok, 7 + 2 * G4)
            lg = LG[:, :].rearrange("p (b g k) -> p b g k", b=NB, g=GROUPS)
            step(dve.tensor_reduce(gm[:, :, :], lg, axis=AX.X, op=ALU.max))
            for m in range(NB):
                ins = dve.max(gv[:, m, :], gm[:, m, :])
            step(ins)
            for m in range(NB):
                ins = dve.max_index(gi[:, m, :], gv[:, m, :], gm[:, m, :])
            step(ins)
            gated(0, 0)
            step(dve.tensor_copy(gif[:, :, :], gi[:, :, :]))
            for k in range(TOPG):
                ins = dve.tensor_tensor(kp[k][:, :, :], io8[:, :].unsqueeze(1).broadcast_to([P, NB, GROUPS]),
                                        gif[:, :, k].unsqueeze(2).broadcast_to([P, NB, GROUPS]), ALU.is_equal)
            step(ins)
            step(dve.tensor_tensor(kp[0][:, :, :], kp[0][:, :, :], kp[1][:, :, :], ALU.add))
            step(dve.tensor_tensor(kp[0][:, :, :], kp[0][:, :, :], kp[2][:, :, :], ALU.add))
            step(dve.tensor_tensor(sc[:, :, :].rearrange("p b (g k) -> p b g k", g=GROUPS), lg,
                                   kp[0][:, :, :].unsqueeze(3).broadcast_to([P, NB, GROUPS, NE // GROUPS]), ALU.mult))
            step(dve.tensor_reduce(smx[:, :], sc[:, :, :], axis=AX.X, op=ALU.max))
            dve.tensor_tensor(sc[:, :, :], sc[:, :, :], smx[:, :].unsqueeze(2).broadcast_to([P, NB, NE]), ALU.subtract).then_inc(sc_ok, 1)
            gated(0, 1)
            gated(0, 2)
            dve.wait_ge(ex_ok, 1)
            step(dve.tensor_reduce(ssum[:, :], ex[:, :, :], axis=AX.X, op=ALU.add))
            step(dve.reciprocal(smx[:, :], ssum[:, :]))
            dve.scalar_tensor_tensor(out=wt[:, :, :], in0=ex[:, :, :], scalar=ROUTE_SCALE,
                                     in1=smx[:, :].unsqueeze(2).broadcast_to([P, NB, NE]), op0=ALU.mult, op1=ALU.mult).then_inc(wt_ok, 1)
            for m in range(4):
                residual(m)
            for m in range(NB):
                ins = dve.max(gv[:, m, :], ex[:, m, :])
            step(ins)
            for m in range(NB):
                ins = dve.max_index(gi[:, m, :], gv[:, m, :], ex[:, m, :])
            step(ins)
            gated(1, 0)
            step(dve.tensor_copy(eih[:, :, :], gi[:, :, :]))
            for k in range(TOPK):
                to = chosen if k == 0 else eq[k % 2]
                step(dve.tensor_tensor(to[:, :, :], io32[:, :].unsqueeze(1).broadcast_to([P, NB, NE]),
                                       eih[:, :, k].unsqueeze(2).broadcast_to([P, NB, NE]), ALU.is_equal))
                if k:
                    step(dve.tensor_tensor(chosen[:, :, :], chosen[:, :, :], to[:, :, :], ALU.add))
            for g in range(G4):
                ins = dve.tensor_copy(chosen4[:, :, g, :], chosen[:, :, :])
            ins.then_inc(chosen_ok, 1)
            gated(1, 1)
            gated(1, 2)
            step(dve.tensor_scalar(own[:, :], own[:, :], 0.0, None, ALU.is_equal))
            step(dve.tensor_tensor(place[:, :, :], io64[:, :].unsqueeze(1).broadcast_to([P, R, 2 * LANE]),
                                   thr[:, :].unsqueeze(2).broadcast_to([P, R, 2 * LANE]), ALU.is_equal))
            dve.tensor_scalar(thr_half[:, :], thr[:, :], 0.5, None, ALU.add).then_inc(cnt_ok, 1)
            for c in range(4):
                dve.wait_ge(cum_mm, c + 1)
                dve.tensor_copy(cum[:, 512 * c:512 * c + 512], TB[c % 2][:, :]).then_inc(cum_ok, 1)
            for m in range(4, 8):
                residual(m)
            dve.wait_ge(cum_ok, 4)

            def count(r):
                step(dve.tensor_scalar(junk, cum[:, :], thr[:, r:r + 1], None, ALU.is_le, ALU.add,
                                       accum_out=tok[:, r:r + 1]))
            n = R - COUNT_ACT
            for f in range(3):
                for r in range(f * n // 3, (f + 1) * n // 3):
                    count(r)
                gated(2, f)
            dve.wait_ge(cnt_act, COUNT_ACT)
            step(dve.tensor_scalar(tok[:, n:R], tok[:, n:R], 0.5, T / 2, ALU.mult, ALU.add))
            dve.tensor_scalar(toki[:, :], tok[:, :], float(T - 1), None, ALU.min).then_inc(toki_ok, 1)
            own_r = own[:, :].unsqueeze(1).broadcast_to([P, R, NE])
            dve.tensor_tensor(tw[:, :, 0, :], own_r, tok[:, :].unsqueeze(2).broadcast_to([P, R, NE]), ALU.mult)
            for m in range(8, 12):
                residual(m)
            for f in range(3):
                gated(3, f)
            for m in range(12, 16):
                residual(m)
            for r in range(R):
                dve.wait_ge(xg_in[r], 16)
            dve.tensor_tensor(tw[:, :, 1, :], own_r, xg[:, :, D:ROW], ALU.mult).then_inc(tw_ok, 1)
            dve.wait_ge(tw_mm, 1)
            step(dve.tensor_copy(twp[:, :, :], LG[:, 0:2 * NE].rearrange("p (a e) -> p a e", a=2)))
            step(dve.tensor_scalar(inv[:, :], twp[0:CAP, 0, :], float(T), pcol[:, :], ALU.is_ge, ALU.mult))
            dve.tensor_tensor(dst[:, :], inv[:, :], twp[0:CAP, 0, :], ALU.add)
            for w in range(2):
                rows = slice(LANE * w, LANE * w + LANE)
                step(dve.tensor_copy(wpair[rows, :], twp[rows, 1, w:NE:2]))

            def weighted(k):
                dve.wait_ge(y_mm, k + 1)
                for w in range(2):
                    at_least(dve, add_in[w], 16 * (k - 2))
                dve.tensor_scalar(ys[k % 3][:, :], YB[k % 2][:, 0:D], wpair[:, k:k + 1], None, ALU.mult).then_inc(ys_ok, 1)
            for k in range(NPAIR):
                dve.wait_ge(es_ok, k + 1)
                at_least(dve, eaT_mm, k - 1)
                dve.tensor_tensor(ea[k % 2][:, :, :], EB[k % 3][:, INNER:2 * INNER].rearrange("p (q m) -> p m q", m=2),
                                  es_[k % 2][:, :, :], ALU.mult).then_inc(ea_ok, 1)
                if k > 1:
                    weighted(k - 2)
            weighted(NPAIR - 2)
            weighted(NPAIR - 1)

        @block.tensor
        def _(pe):
            pe.wait_ge(gw_in, 16)
            for c in range(DK):
                ins = pe.transpose(TB[0][:, c * NE:c * NE + NE], gw[:, c * P:c * P + P], identf[0:NE, 0:NE])
            ins.then_inc(gwT_mm, 1)
            pe.wait_ge(gwT_ok, 1)

            def logits(m):
                pe.wait_ge(hT_ok, m + 1)
                for c in range(DK):
                    ins = pe.matmul(LG[:, m * NE:m * NE + NE], hT[:, c, m * P:m * P + P], gwT[:, c, :], start=(c == 0), stop=(c == DK - 1))
                ins.then_inc(lg_mm, 1)
            for m in range(NB):
                pe.wait_ge(h_ok, m + 1)
                at_least(pe, hT_ok, m - 1)
                for c in range(DK):
                    ins = pe.transpose(TB[m % 2][:, c * P:c * P + P], h[m % 2][:, c * P:c * P + P], identf[:, :])
                ins.then_inc(hT_mm, 1)
                if m:
                    logits(m - 1)
            logits(NB - 1)
            pe.wait_ge(w2_in, 48)

            def up(k, f):
                i, (a, n) = 3 * k + f, FC[f]
                at_least(pe, ac_ok, i - 1)
                for w in range(2):
                    for c in range(DK):
                        ins = pe.matmul(GU[2 * (i % 2) + w][0:n, :], WSG[:, c, w * SHARED + a:w * SHARED + a + n],
                                        hT[:, c, 512 * k:512 * k + 512], start=(c == 0), stop=(c == DK - 1))
                ins.then_inc(up_mm, 1)

            def down(m):
                k, j = m // 4, m % 4
                pe.wait_ge(ac_ok, 3 * k + 3)
                at_least(pe, ro_ok, m)
                for f in range(3):
                    n = FC[f][1]
                    ins = pe.matmul(DN[:, 0:D], ac[k % 2][0:n, f, j * P:j * P + P], WSD[0:n, f, :], start=(f == 0), stop=(f == 2))
                ins.then_inc(dn_mm, 1)

            def cumulate(c):
                at_least(pe, cum_ok, c - 1)
                for i in range(4 * c + 4):
                    a = max(i - 4 * c, 0) * P
                    rhs = tri[:, 0:512 - a] if i >= 4 * c else ones4[:, :]
                    ins = pe.matmul(TB[c % 2][:, a:512], chosen4[:, i, :, :], rhs, start=(i == 0), stop=(i == 4 * c + 3))
                ins.then_inc(cum_mm, 1)

            for f in range(3):
                up(0, f)
            up(1, 0)
            for m in range(4):
                down(m)
            up(1, 1)
            pe.wait_ge(chosen_ok, 1)
            for c in range(2):
                cumulate(c)
            up(1, 2)
            for c in range(2, 4):
                cumulate(c)
            up(2, 0)
            for m in range(4, 8):
                down(m)
            up(2, 1)
            up(2, 2)
            up(3, 0)
            for m in range(8, 12):
                down(m)
            up(3, 1)
            up(3, 2)
            for m in range(12, 16):
                down(m)
            for r in range(R):
                pe.wait_ge(xg_in[r], 16)
                at_least(pe, xb_ok, r - 1)
                for c in range(DK):
                    ins = pe.transpose(TB[r % 2][:, c * P:c * P + P], xg[:, r, c * P:c * P + P], identf[:, :])
                ins.then_inc(xb_mm, 1)
            pe.wait_ge(tw_ok, 1)
            for r in range(R):
                ins = pe.matmul(LG[:, 0:2 * NE], place[:, r, :], tw[:, r, :, :], start=(r == 0), stop=(r == R - 1))
            ins.then_inc(tw_mm, 1)
            pe.wait_ge(xb_ok, R)

            def pair_up(k):
                for c in range(DK):
                    for e in (2 * k, 2 * k + 1):
                        lane = slice(LANE * (e % 2), LANE * (e % 2) + LANE)
                        ins = pe.matmul(EB[k % 3][lane, 0:2 * INNER], xbT[:, c, e * CAP:e * CAP + LANE], ring.gu[:, e % RESIDENT, c, :],
                                        start=(c == 0), stop=(c == DK - 1), tile_position=(0, LANE * (e % 2)))
                ins.then_inc(eup_mm, 1)

            def pair_turn(k):
                pe.wait_ge(ea_ok, k + 1)
                at_least(pe, eaT_ok, k - 1)
                for m in range(2):
                    ins = pe.transpose(ET[k % 2][0:IH, m * P:m * P + P], ea[k % 2][:, m, :], identf[:, :])
                ins.then_inc(eaT_mm, 1)

            def pair_down(k):
                pe.wait_ge(eaT_ok, k + 1)
                at_least(pe, ys_ok, k - 1)
                for m in range(2):
                    for e in (2 * k, 2 * k + 1):
                        lane = slice(LANE * (e % 2), LANE * (e % 2) + LANE)
                        ins = pe.matmul(YB[k % 2][lane, 0:D], eaT[k % 2][:, m, lane], ring.dn[:, e % RESIDENT, m, :],
                                        start=(m == 0), stop=(m == 1), tile_position=(0, LANE * (e % 2)))
                ins.then_inc(y_mm, 1)
            for k in range(NPAIR):
                if 2 * k % LOT == 0:
                    pe.wait_ge(ring.lot_in[2 * k % RESIDENT // LOT], ring.LOADS * (1 + 2 * k // RESIDENT))
                at_least(pe, ea_ok, k - 2)
                pair_up(k)
                if k:
                    pair_turn(k - 1)
                if k > 1:
                    pair_down(k - 2)
            pair_turn(NPAIR - 1)
            pair_down(NPAIR - 2)
            pair_down(NPAIR - 1)


_INS = ["x", "ctx_1024", "fside_BxSx2_0", "L0_xattn_Wq", "L0_xattn_Wkv", "L0_xattn_Wout", "L0_xattn_bout",
        "L0_ffn_gate_w", "L0_ffn_w_gate_up", "L0_ffn_w_down", "L0_ffn_ws_gate_up", "L0_ffn_ws_down"]


def kernel(**inputs):
    import concourse.bacc as bacc
    from concourse.bass_utils import run_bass_kernel_spmd

    nc = bacc.Bacc("TRN2", target_bir_lowering=False, num_devices=1)
    arrays, args = {}, []
    for name in _INS:
        a = np.ascontiguousarray(inputs[name])
        arrays[f"in_{name}"] = a
        args.append(nc.dram_tensor(f"in_{name}", a.shape, F32, kind="ExternalInput").ap())
    out = nc.dram_tensor("out", (T + CAP, D), F32, kind="ExternalOutput").ap()
    build(nc, *args, out)
    r = run_bass_kernel_spmd(nc, [arrays], core_ids=[0])
    return r.results[0]["out"][:T].reshape(NB, P, D)
```

```python
from contextlib import ExitStack

import numpy as np

import concourse.bass as bass
from concourse import mybir

ALU = mybir.AluOpType
ACT = mybir.ActivationFunctionType
AX = mybir.AxisListType
F32 = mybir.dt.float32
F16 = mybir.dt.float16
U32 = mybir.dt.uint32

P = 128
NB, D, DC = 16, 256, 128
NH, HD = 32, 8
QUADS, SLOT = NH // 4, 32
DK = D // P
MAXROW = 3 * HD
SCALE = float(1.0 / np.sqrt(np.float32(HD)))
EPS = 1e-5
TWO_PI = 6.283185
BIG = 12582912.0
NE, INNER, TOPK, CAP = 32, 176, 6, 48
GROUPS, TOPG = 8, 3
SHARED = 2 * INNER
ROUTE_SCALE = 16.0
WUP = 64.0
RESIDENT = 10
IH = INNER // 2
T = NB * P
NPAIR, LANE = NE // 2, 64
COUNT_ACT = 4


class Batch:

    def __init__(self, half, par):
        self.half, self.par = half + par // 2, par % 2
        self.n = 2 * self.half + self.par

    def __add__(self, k):
        return Batch(self.half, self.par + k) if k >= 0 or self.par + k >= 0 else Batch(self.half - 1, self.par + k + 2)


def at_least(eng, sem, count):
    if not isinstance(count, int) or count > 0:
        eng.wait_ge(sem, count)


def build(nc, x, ctx_in, pos, wq, wkv, wout, bout, gate_w, w_gu, w_dn, ws_gu, ws_dn, out):
    with ExitStack() as es:
        def keep(name, shape, dt=F32):
            return es.enter_context(nc.sbuf_tensor(name, shape, dt))

        def sem(name):
            return es.enter_context(nc.semaphore(name))

        X = keep("X", [P, NB, D])
        identf = keep("identf", [P, P])
        st2 = keep("st2", [P, NB, 6])
        ring = Ring(nc, keep, sem, w_gu, w_dn)
        ahead = Ahead(nc, keep, sem, gate_w, ws_gu, ws_dn)
        attention(nc, sem, X, identf, st2, ring, ahead, x, ctx_in, pos, wq, wkv, wout, bout)
        mixture(nc, sem, X, identf, st2, ring, ahead, out)


class Ring:

    def __init__(self, nc, keep, sem, w_gu, w_dn):
        gu = keep("ring_gu", [P, RESIDENT, 2, DK, 2 * INNER])
        dn = keep("ring_dn", [IH, RESIDENT, 2, 2, D])
        self.gu, self.dn = ([t[:, n] for n in range(RESIDENT)] for t in (gu, dn))
        self.pair_in = [sem(f"pair_in{n}") for n in range(RESIDENT)]
        self.sem = sem
        self.w_gu = w_gu.rearrange("e (c p) f -> p e c f", p=P)
        self.w_dn = w_dn.rearrange("e (p m) n -> p e m n", m=2)

    def more(self, memory):
        gu, dn = 2 * DK * 2 * INNER, 2 * 2 * D
        self.gu.append(memory[:, 0:gu].rearrange("p (e c f) -> p e c f", e=2, c=DK))
        self.dn.append(memory[0:IH, gu:gu + dn].rearrange("p (e m n) -> p e m n", e=2, m=2))
        self.pair_in.append(self.sem(f"pair_in{len(self.pair_in)}"))

    def load(self, eng, pair):
        place = pair % len(self.gu)
        for e in range(2):
            eng.dma_start(self.gu[place][:, e], self.w_gu[:, 2 * pair + e]).then_inc(self.pair_in[place], 16)
        eng.dma_start(self.dn[place], self.w_dn[:, 2 * pair:2 * pair + 2]).then_inc(self.pair_in[place], 16)

    def wait(self, eng, pair):
        eng.wait_ge(self.pair_in[pair % len(self.gu)], 48 * (1 + pair // len(self.gu)))


class Ahead:

    def __init__(self, nc, keep, sem, gate_w, ws_gu, ws_dn):
        self.gw = keep("gw", [NE, D])
        self.WSG = keep("WSG", [P, DK, 2, 2 * SHARED], F16)
        self.WSD = keep("WSD", [P, 3, D])
        self.zero = keep("zero", [P, D])
        self.gw_in, self.wsg_in, self.w2_in, self.zero_ok = sem("gw_in"), sem("wsg_in"), sem("w2_in"), sem("zero_ok")
        self.wsg_hi, self.wsg_lo = sem("wsg_hi"), sem("wsg_lo")
        self.sources = gate_w, ws_gu, ws_dn

    def load(self, eng, part, raw):
        gate_w, ws_gu, ws_dn = self.sources
        if part < DK:
            eng.dma_start(raw[:, part, :], ws_gu[part * P:part * P + P]).then_inc(self.wsg_in, 16)
        if part == DK:
            eng.dma_start(self.WSD[:, 0:2, :], ws_dn[0:2 * P].rearrange("(c p) n -> p c n", p=P)).then_inc(self.w2_in, 16)
        if part == DK + 1:
            eng.dma_start(self.WSD[0:SHARED - 2 * P, 2, :], ws_dn[2 * P:SHARED]).then_inc(self.w2_in, 16)
            eng.dma_start(self.gw[:, :], gate_w).then_inc(self.gw_in, 16)

    def split_hi(self, act, raw):
        act.wait_ge(self.wsg_in, 16 * DK)
        act.activation(self.WSG[:, :, 0, :], raw[:, :, :], ACT.Copy, scale=WUP).then_inc(self.wsg_hi, 1)

    def split_lo(self, dve, raw):
        dve.wait_ge(self.wsg_hi, 1)
        dve.scalar_tensor_tensor(out=self.WSG[:, :, 1, :], in0=raw[:, :, :], scalar=WUP, in1=self.WSG[:, :, 0, :],
                                 op0=ALU.mult, op1=ALU.subtract).then_inc(self.wsg_lo, 1)

    PARTS = DK + 2


def attention(nc, sem, X, identf, st2, ring, ahead, x, ctx_in, pos, wq, wkv, wout, bout):
    with ExitStack() as es:
        def sb(name, shape, dt=F32):
            return es.enter_context(nc.sbuf_tensor(name, shape, dt))

        POS = sb("POS", [P, NB, 2])
        WQ = sb("WQ", [P, DK, D])
        WKV = sb("WKV", [P, 2 * D])
        WO = sb("WO", [P, DK, D])
        BO = sb("BO", [P, D])
        identh = sb("identh", [P, P], F16)
        CT = [sb(f"CT{i}", [P, DC]) for i in range(2)]
        xn = sb("xn", [P, D])
        xcT = [sb(f"xcT{i}", [P, 3, P]) for i in range(2)]
        t1 = sb("t1", [P, 2 * D])
        t2 = sb("t2", [P, 2 * D])
        rot = sb("rot", [P, 2 * D])
        tokst = [sb(f"tokst{i}", [P, 2, NH, SLOT], F16) for i in range(2)]
        qst = [sb(f"qst{i}", [P, QUADS, P], F16) for i in range(2)]
        kT = sb("kT", [P, QUADS, P], F16)
        kz = [sb(f"kz{i}", [P, 4, QUADS, P], F16) for i in range(2)]
        V = [sb(f"V{i}", [P, NH, SLOT]) for i in range(2)]
        mx = [sb(f"mx{i}", [P, 4, 2], F16) for i in range(2)]
        mxs = [sb(f"mxs{i}", [8, P], F16) for i in range(2)]
        pw = [sb(f"pw{i}", [P, 4 * P]) for i in range(2)]
        OT = [sb(f"OT{i}", [P, 4, P]) for i in range(2)]
        rec = sb("rec", [P, 2, NH // 2])
        attn = sb("attn", [P, D])
        attnT = sb("attnT", [P, DK, P])
        st1 = sb("st1", [P, NB, 6])
        mv1 = sb("mv1", [P, NB, 2])
        rs1 = sb("rs1", [P, NB, 1])
        nb1 = sb("nb1", [P, NB, 1])
        ang = sb("ang", [P, 2, NB, 2, 2])
        turns = sb("turns", [P, 2, NB, 2, 2])
        raw_wsg = sb("raw_wsg", [P, DK, 2 * SHARED])
        RC = sb("RC", [P, NB, 4, 2])
        RS = sb("RS", [P, NB, 4, 2])
        bank = [es.enter_context(nc.psum_tensor(f"bank{i}", [P, 512], F32)) for i in range(8)]
        SB, STB, OB, M0, M1 = bank[0:2], bank[2:4], bank[4:6], bank[6], bank[7]

        x_in = [sem(f"x_in{i}") for i in range(4)]
        pos_in, w_in, bo_in = sem("pos_in"), sem("w_in"), sem("bo_in")
        ctx_in_s = [sem(f"ctx_in{i}") for i in range(2)]
        consts, consts2, kz_zero = sem("consts"), sem("consts2"), sem("kz_zero")
        stat1, mv1_ok, std1, rs1_ok = sem("stat1"), sem("mv1_ok"), sem("std1"), sem("rs1_ok")
        turn_s, sin_s, rope_tab = sem("turn_s"), sem("sin_s"), sem("rope_tab")
        xn_ok, x_biased = sem("xn_ok"), sem("x_biased")
        xcT_mm, xcT_ok = sem("xcT_mm"), sem("xcT_ok")
        qk_mm, rope_ok, tokst_ok = sem("qk_mm"), sem("rope_ok"), sem("tokst_ok")
        rot_ok, hi_ok = ([sem(f"{n}_{w}") for w in "qk"] for n in ("rot_ok", "hi_ok"))
        qstT_mm, kstT_mm, qst_ok, kT_ok = sem("qstT_mm"), sem("kstT_mm"), sem("qst_ok"), sem("kT_ok")
        kz_in = [sem(f"kz_in{i}") for i in range(2)]
        v_mm, v_ok = sem("v_mm"), sem("v_ok")
        s_mm, max_ok, mxT_mm, mxs_ok = sem("s_mm"), sem("max_ok"), sem("mxT_mm"), sem("mxs_ok")
        mr_in = [sem(f"mr_in{i}") for i in range(2)]
        st_mm, exp_ok, pv_mm, OT_ok = sem("st_mm"), sem("exp_ok"), sem("pv_mm"), sem("OT_ok")
        ob_mm, rec_ok, attn_ok = sem("ob_mm"), sem("rec_ok"), sem("attn_ok")
        attnT_mm, attnT_ok, wo_mm, x1_ok, st2_ok = (sem(n) for n in ("attnT_mm", "attnT_ok", "wo_mm", "x1_ok", "st2_ok"))

        xr = x.rearrange("b p d -> p b d")

        def periods(eng, period):
            for n in range(-3, 2):
                period(Batch(n // 2, n % 2))
            with eng.Fori(0, 5) as i:
                for u in range(2):
                    period(Batch(i, 2 + u))
            for n in range(12, NB + 1):
                period(Batch(n // 2, n % 2))

        def inside(b, lo=0, hi=NB - 1):
            return not isinstance(b.n, int) or lo <= b.n <= hi

        def split(eng, m):
            at_least(eng, rope_ok, m.n + 1)
            at_least(eng, tokst_ok, 2 * m.n)
            for w in (1, 0):
                part = slice(w * D, w * D + D)
                eng.tensor_tensor(rot[:, part], t1[:, part], t2[:, part], ALU.add).then_inc(rot_ok[w], 1)
            for w in (1, 0):
                eng.wait_ge(consts2, 6)
                at_least(eng, rot_ok[w], m.n + 1)
                hi = tokst[m.par][:, w, :, 0:HD]
                r = rot[:, w * D:w * D + D].rearrange("p (h d) -> p h d", d=HD)
                eng.tensor_copy(hi, r).then_inc(hi_ok[w], 1)
                eng.wait_ge(consts2, 6)
                at_least(eng, hi_ok[w], m.n + 1)
                a = (2 - w) * HD
                eng.tensor_tensor(tokst[m.par][:, w, :, a:a + HD], r, hi, ALU.subtract)
                a = (1 + w) * HD
                eng.tensor_copy(tokst[m.par][:, w, :, a:a + HD], hi).then_inc(tokst_ok, 1)

        block = es.enter_context(nc.Block())

        @block.sync
        def _(sp):
            sp.dma_start(POS[:, :, :], pos.rearrange("b p a -> p b a")).then_inc(pos_in, 16)
            for c in range(4):
                sp.dma_start(X[:, 4 * c:4 * c + 4, :], xr[:, 4 * c:4 * c + 4, :]).then_inc(x_in[c], 16)
                if c == 0:
                    sp.dma_start(CT[0][:, :], ctx_in[0]).then_inc(ctx_in_s[0], 16)
                    sp.dma_start(WQ[:, :, :], wq.rearrange("(c p) n -> p c n", p=P)).then_inc(w_in, 16)
                    sp.dma_start(WKV[:, :], wkv).then_inc(w_in, 16)
                    sp.dma_start(WO[:, :, :], wout.rearrange("(c p) n -> p c n", p=P)).then_inc(w_in, 16)
                    sp.dma_start(BO[:, :], bout.rearrange("(a n) -> a n", a=1).broadcast_to([P, D])).then_inc(bo_in, 16)

            def period(b):
                m1, m4 = b + 1, b + 4
                if inside(m1):
                    if isinstance(b.n, int) and b.n < 1:
                        sp.wait_ge(kz_zero, 2)
                        sp.wait_ge(kT_ok, m1.n + 1)
                    else:
                        sp.wait_ge(exp_ok, QUADS * b.n)
                    for j in range(4):
                        sp.dma_start(kz[m1.par][32 * j:32 * j + 32, j, :, :],
                                     kT[32 * j:32 * j + 32, :, :]).then_inc(kz_in[m1.par], 16)
                for g in (1, 3, 5, 7):
                    who, half = (b, (g + 3) // 2) if g < 5 else (m1, (g - 5) // 2)
                    if inside(who):
                        k = 4 * who.n + half
                        sp.wait_ge(mxs_ok, k + 1)
                        sp.dma_start(qst[who.par][MAXROW:P:SLOT, 2 * half:2 * half + 2, :],
                                     mxs[half % 2][:, :]).then_inc(mr_in[half % 2], 16)
                    if g == 1 and inside(m4):
                        at_least(sp, xcT_mm, m4.n - 1)
                        sp.wait_ge(consts, 2)
                        sp.dma_start(CT[m4.par][:, :], ctx_in[m4.n]).then_inc(ctx_in_s[m4.par], 16)
            periods(sp, period)

        @block.gpsimd
        def _(pool):
            pool.memset(identf[:, :], 0.0).then_inc(consts, 1)
            pool.memset(identh[:, :], 0.0).then_inc(consts, 1)
            pool.wait_ge(consts, 2)
            for m in (identf, identh):
                pool.affine_select(out=m[:, :], in_=m[:, :], compare_op=ALU.not_equal, fill=1.0, base=0,
                                   pattern=[[-1, P]], channel_multiplier=1).then_inc(consts2, 1)
            for i in range(2):
                pool.memset(tokst[i][:, :, :, MAXROW:SLOT], 0.0).then_inc(consts2, 1)
            pool.wait_ge(consts2, 4)
            for i in range(2):
                pool.memset(tokst[i][:, 1, :, MAXROW:MAXROW + 1], 1.0).then_inc(consts2, 1)
            for i in range(2):
                pool.memset(V[i][:, :, HD + 1:SLOT], 0.0).then_inc(consts, 1)
                pool.memset(V[i][:, :, HD:HD + 1], 1.0).then_inc(consts, 1)
            pool.memset(ahead.zero[:, :], 0.0).then_inc(ahead.zero_ok, 1)
            for i in range(2):
                pool.memset(kz[i][:, :, :, :], 0.0).then_inc(kz_zero, 1)

            def add_bias(m):
                at_least(pool, xn_ok, m.n + 1)
                pool.tensor_tensor(X[:, m.n, :], X[:, m.n, :], BO[:, :], ALU.add).then_inc(x_biased, 1)

            pool.wait_ge(bo_in, 16)

            def period(b):
                if inside(b + 3):
                    add_bias(b + 3)
                    if not (isinstance(b.n, int) and b.n == -3):
                        split(pool, b + 3)
            periods(pool, period)

        @block.scalar
        def _(act):
            act.wait_ge(turn_s, 5)
            act.activation(ang[:, :, :, :, :], turns[:, :, :, :, :], ACT.Sin, scale=TWO_PI).then_inc(sin_s, 1)

            def std(a, e, k):
                act.wait_ge(mv1_ok, 2 * k + 2)
                act.activation(rs1[:, a:e, 0], nb1[:, a:e, 0], ACT.Sqrt).then_inc(std1, 1)
            std(0, 4, 0)

            def norm(m):
                act.wait_ge(rs1_ok, 2 if isinstance(m.n, int) and m.n < 4 else 4)
                at_least(act, xcT_mm, m.n)
                act.activation(xn[:, :], X[:, m.n, :], ACT.Identity, bias=nb1[:, m.n, :],
                               scale=rs1[:, m.n, :]).then_inc(xn_ok, 1)

            def evac_xcT(m):
                at_least(act, xcT_mm, m.n + 1)
                at_least(act, v_mm, m.n - 1)
                act.copy(xcT[m.par][:, :, :], M1[:, 0:3 * P].rearrange("p (c t) -> p c t", c=3)).then_inc(xcT_ok, 1)

            norm(Batch(0, 0))

            def period(b):
                m1, m2, m3, m4, o = b + 1, b + 2, b + 3, b + 4, b + -1
                for g in range(QUADS):
                    if inside(b):
                        act.wait_ge(st_mm, QUADS * b.n + g + 1)
                        at_least(act, pv_mm, QUADS * b.n + g - 1)
                        act.activation(pw[g % 2][:, :], STB[g % 2][:, :], ACT.Exp, scale=SCALE).then_inc(exp_ok, 1)
                    if g == 0 and inside(m1):
                        at_least(act, v_mm, m1.n + 1)
                        at_least(act, pv_mm, QUADS * b.n)
                        act.copy(V[m1.par][:, :, 0:HD], M0[:, 0:D].rearrange("p (h d) -> p h d", d=HD)).then_inc(v_ok, 1)
                    if g == 0 and inside(m3):
                        evac_xcT(m3)
                    if g == 1 and inside(m1):
                            at_least(act, qstT_mm, m1.n + 1)
                            at_least(act, st_mm, QUADS * b.n)
                            act.copy(qst[m1.par][:, :, :], M0[:, :].bitcast(F16).rearrange("p (q t) -> p q t", q=QUADS)).then_inc(qst_ok, 1)
                    if g == 2 and inside(o):
                        evac_OT(o, 1)
                    if g == 4 and inside(m4):
                        norm(m4)
                    if g == 4 and isinstance(b.n, int) and b.n == -1:
                        std(4, NB, 1)
                    if g in (3, 6) and isinstance(b.n, int) and b.n < 2:
                        ring.load(act, 2 * (b.n + 3) + g // 6)
                    if g in (3, 6) and isinstance(b.n, int) and 12 <= b.n < 12 + ahead.PARTS // 2:
                        ahead.load(act, 2 * (b.n - 12) + g // 6, raw_wsg)
                    if g == 7 and isinstance(b.n, int) and b.n == 14:
                        ahead.split_hi(act, raw_wsg)
                    if g == 5 and inside(b):
                        evac_OT(b, 0)
                    if g == 5 and inside(o):
                        act.wait_ge(attnT_mm, o.n + 1)
                        at_least(act, wo_mm, o.n)
                        act.copy(attnT[:, :, :], M0[:, D:2 * D].rearrange("p (c t) -> p c t", c=DK)).then_inc(attnT_ok, 1)
                    if g == 6 and inside(m2):
                        at_least(act, kstT_mm, m2.n + 1)
                        if inside(m1):
                            act.wait_ge(kz_in[m1.par], 64 * (m1.half + 1))
                        act.copy(kT[:, :, :], M1[:, :].bitcast(F16).rearrange("p (q t) -> p q t", q=QUADS)).then_inc(kT_ok, 1)

            def evac_OT(m, half):
                act.wait_ge(pv_mm, QUADS * m.n + 4 * half + 4)
                at_least(act, ob_mm, 2 * m.n + half - 1)
                act.copy(OT[half][:, :, :], OB[half][:, :].rearrange("p (q t) -> p q t", q=4)).then_inc(OT_ok, 1)
            periods(act, period)

        @block.vector
        def _(dve):
            freq = [float(np.float32(10000.0) ** np.float32(-f / 2)) for f in range(2)]
            dve.wait_ge(pos_in, 16)
            for f in range(2):
                for c in range(2):
                    dve.tensor_scalar(turns[:, c, :, :, f], POS[:, :, :], freq[f] / (2 * np.pi), 0.25 * c,
                                      ALU.mult, ALU.add).then_inc(turn_s, 1)
            dve.wait_ge(turn_s, 4)
            dve.tensor_scalar(ang[:, :, :, :, :], turns[:, :, :, :, :], BIG, BIG, ALU.add, ALU.subtract).then_inc(rope_tab, 1)
            dve.wait_ge(rope_tab, 1)
            dve.tensor_tensor(turns[:, :, :, :, :], turns[:, :, :, :, :], ang[:, :, :, :, :], ALU.subtract).then_inc(turn_s, 1)

            def statistics(a, e, k):
                for j in range(a, e):
                    if j % 4 == 0:
                        dve.wait_ge(x_in[j // 4], 16)
                    dve.bn_stats(st1[:, j, :], X[:, j, :]).then_inc(stat1, 1)
                for j in range(a, e):
                    dve.wait_ge(stat1, j + 1)
                    ins = dve.bn_aggr(mv1[:, j, :], st1[:, j, :])
                ins.then_inc(mv1_ok, 1)
                dve.wait_ge(mv1_ok, 2 * k + 1)
                dve.tensor_scalar(nb1[:, a:e, 0], mv1[:, a:e, 1], EPS, None, ALU.add).then_inc(mv1_ok, 1)
                if k == 0:
                    dve.wait_ge(sin_s, 1)
                    sin = ang[:, 0].rearrange("p b a f -> p b (a f)")
                    cos = ang[:, 1].rearrange("p b a f -> p b (a f)")
                    for r in range(2):
                        dve.tensor_copy(RC[:, :, :, r], cos)
                        dve.tensor_scalar(RS[:, :, :, r], sin, -1.0 if r == 0 else 1.0, None, ALU.mult).then_inc(rope_tab, 1)
                dve.wait_ge(std1, k + 1)
                dve.reciprocal(rs1[:, a:e, 0], rs1[:, a:e, 0]).then_inc(rs1_ok, 1)
                dve.wait_ge(rs1_ok, 2 * k + 1)
                dve.scalar_tensor_tensor(out=nb1[:, a:e, 0], in0=mv1[:, a:e, 0], scalar=-1.0, in1=rs1[:, a:e, 0],
                                         op0=ALU.mult, op1=ALU.mult).then_inc(rs1_ok, 1)
            statistics(0, 4, 0)
            dve.wait_ge(rope_tab, 3)

            def rope_cos(m):
                at_least(dve, qk_mm, m.n + 1)
                at_least(dve, rot_ok[0], m.n)
                o1 = t1[:, :].rearrange("p (x a) -> p x a", a=8)
                rc = RC[:, m.n].rearrange("p a r -> p (a r)").unsqueeze(1).broadcast_to([P, 2 * NH, 8])
                dve.tensor_tensor(o1, M1[:, :].rearrange("p (x a) -> p x a", a=8), rc, ALU.mult)

            def rope_sin(m):
                qk = M1[:, :].rearrange("p (x a r) -> p x a r", a=4, r=2)
                o2 = t2[:, :].rearrange("p (x a r) -> p x a r", a=4, r=2)
                for r in range(2):
                    rs = RS[:, m.n, :, r].unsqueeze(1).broadcast_to([P, 2 * NH, 4])
                    ins = dve.tensor_tensor(o2[:, :, :, r], qk[:, :, :, 1 - r], rs, ALU.mult)
                ins.then_inc(rope_ok, 1)

            def row_max(m, u):
                dve.wait_ge(s_mm, QUADS * m.n + u + 1)
                if not (isinstance(m.n, int) and 4 * m.n + u // 2 < 2):
                    dve.wait_ge(mxT_mm, 4 * m.n + u // 2 - 1)
                dve.tensor_reduce(mx[u // 2 % 2][:, :, u % 2], SB[u % 2][:, :].rearrange("p (j t) -> p j t", j=4),
                                  axis=AX.X, op=ALU.max, negate=True).then_inc(max_ok, 1)

            def evac_max(m, half):
                k = 4 * m.n + half
                dve.wait_ge(mxT_mm, k + 1)
                at_least(dve, mr_in[half % 2], 16 * (2 * m.n + half // 2))
                dve.tensor_copy(mxs[half % 2][:, :], SB[1][0:8, 0:P // 2].bitcast(F16)).then_inc(mxs_ok, 1)

            def normalise(m, half):
                at_least(dve, ob_mm, 2 * m.n + half + 1)
                ob = OB[half][:, :].rearrange("p (h s) -> p h s", s=SLOT)
                at_least(dve, attn_ok, 2 * m.n + half)
                dve.reciprocal(rec[:, half, :], ob[:, :, HD]).then_inc(rec_ok, 1)
                at_least(dve, attnT_mm, m.n)
                dve.wait_ge(rec_ok, 2 * m.n + half + 1)
                dve.tensor_tensor(attn[:, half * P:half * P + P].rearrange("p (h d) -> p h d", d=HD), ob[:, :, 0:HD],
                                  rec[:, half, :].unsqueeze(2).broadcast_to([P, NH // 2, HD]), ALU.mult).then_inc(attn_ok, 1)

            def period(b):
                m1, m3, o = b + 1, b + 3, b + -1
                for g in range(QUADS):
                    if g == 7 and inside(o):
                        dve.wait_ge(wo_mm, o.n + 1)
                        dve.wait_ge(x_biased, o.n + 1)
                        dve.tensor_tensor(X[:, o.n, :], M0[:, 0:D], X[:, o.n, :], ALU.add).then_inc(x1_ok, 1)
                    if g == 3 and inside(m3):
                        rope_cos(m3)
                    if g % 2 == 1:
                        who, half = (b, (g + 3) // 2) if g < 5 else (m1, (g - 5) // 2)
                        if inside(who):
                            evac_max(who, half)
                    who, u = (b, g + 5) if g < 3 else (m1, g - 3)
                    if inside(who):
                        row_max(who, u)
                    if g == 7 and inside(o):
                        dve.wait_ge(x1_ok, o.n + 1)
                        dve.wait_ge(rope_tab, 3)
                        dve.bn_stats(st2[:, o.n, :], X[:, o.n, :]).then_inc(st2_ok, 1)
                    if g == 0 and inside(o):
                        normalise(o, 0)
                    if g == 3 and inside(o):
                        normalise(o, 1)
                    if g == 4 and inside(m3):
                        rope_sin(m3)
                    if g == 4 and isinstance(b.n, int) and b.n == -3:
                        split(dve, m3)
                    if g == 4 and isinstance(b.n, int) and b.n == -2:
                        statistics(4, NB, 1)
                    if g == 7 and isinstance(b.n, int) and b.n == 15:
                        ahead.split_lo(dve, raw_wsg)
            periods(dve, period)

        @block.tensor
        def _(pe):
            pe.wait_ge(consts2, 2)

            def transpose_xc(m):
                at_least(pe, xn_ok, m.n + 1)
                pe.wait_ge(ctx_in_s[m.par], 16 * (m.half + 1))
                at_least(pe, rope_ok, m.n)
                at_least(pe, kT_ok, m.n - 1)
                for c in range(DK):
                    pe.transpose(M1[:, c * P:c * P + P], xn[:, c * P:c * P + P], identf[:, :])
                pe.transpose(M1[:, DK * P:DK * P + P], CT[m.par][:, :], identf[:, :]).then_inc(xcT_mm, 1)

            def project_k(m):
                at_least(pe, xcT_ok, m.n + 1)
                pe.matmul(M1[:, D:2 * D], xcT[m.par][:, DK, :], WKV[:, 0:D], start=True, stop=True)

            def project_q(m):
                for c in range(DK):
                    ins = pe.matmul(M1[:, 0:D], xcT[m.par][:, c, :], WQ[:, c, :], start=(c == 0), stop=(c == DK - 1))
                ins.then_inc(qk_mm, 1)

            def transpose_q(m):
                at_least(pe, tokst_ok, 2 * m.n + 2)
                at_least(pe, v_ok, m.n + 1)
                for q in range(QUADS):
                    ins = pe.transpose(M0[:, q * 64:q * 64 + 64].bitcast(F16), tokst[m.par][:, 0, 4 * q:4 * q + 4, :], identh[:, :])
                ins.then_inc(qstT_mm, 1)

            def transpose_k(m):
                at_least(pe, tokst_ok, 2 * m.n + 1)
                at_least(pe, rope_ok, min(m.n + 2, NB) if isinstance(m.n, int) else m.n + 2)
                for q in range(QUADS):
                    ins = pe.transpose(M1[:, q * 64:q * 64 + 64].bitcast(F16), tokst[m.par][:, 1, 4 * q:4 * q + 4, :], identh[:, :])
                ins.then_inc(kstT_mm, 1)

            def project_v(m):
                at_least(pe, x1_ok, m.n - 2)
                pe.matmul(M0[:, 0:D], xcT[m.par][:, DK, :], WKV[:, D:2 * D], start=True, stop=True).then_inc(v_mm, 1)

            def logits_q(m, u):
                if u == 0:
                    at_least(pe, qst_ok, m.n + 1)
                    pe.wait_ge(kz_in[m.par], 64 * (m.half + 1))
                at_least(pe, max_ok, QUADS * m.n + u - 1)
                if u % 2:
                    at_least(pe, mxs_ok, 4 * m.n + u // 2)
                pe.matmul(SB[u % 2][:, :], qst[m.par][:, u, :], kz[m.par][:, :, u, :], start=True, stop=True).then_inc(s_mm, 1)

            def transpose_max(m, half):
                pe.wait_ge(max_ok, QUADS * m.n + 2 * half + 2)
                pe.transpose(SB[1][0:8, 0:P // 2].bitcast(F16), mx[half % 2][:, :, :], identh[:, :]).then_inc(mxT_mm, 1)

            def logits_k(m, g):
                at_least(pe, exp_ok, QUADS * m.n + g - 1)
                if g % 2 == 0:
                    half = g // 2
                    pe.wait_ge(mr_in[half % 2], 16 * (2 * m.n + half // 2 + 1))
                for j in range(4):
                    ins = pe.matmul(STB[g % 2][:, j * P:j * P + P], kz[m.par][:, j, g, :], qst[m.par][:, g, :],
                                    start=True, stop=True)
                ins.then_inc(st_mm, 1)

            def weigh_values(m, g):
                pe.wait_ge(exp_ok, QUADS * m.n + g + 1)
                if isinstance(m.n, int) and m.n == 0 and g == 0:
                    pe.wait_ge(consts, 6)
                if g == 0:
                    at_least(pe, v_ok, m.n + 1)
                if g % 4 == 0:
                    at_least(pe, attn_ok, 2 * m.n + g // 4 - 1)
                for j in range(4):
                    ins = pe.matmul(OB[g // 4][32 * j:32 * j + 32, (g % 4) * P:(g % 4) * P + P], V[m.par][:, 4 * g + j, :],
                                    pw[g % 2][:, j * P:j * P + P], start=True, stop=True, tile_position=(0, 32 * j))
                ins.then_inc(pv_mm, 1)

            def transpose_outputs(m, half):
                pe.wait_ge(OT_ok, 2 * m.n + half + 1)
                for q in range(4):
                    ins = pe.transpose(OB[half][:, q * P:q * P + P], OT[half][:, q, :], identf[:, :])
                ins.then_inc(ob_mm, 1)

            def transpose_attn(m):
                pe.wait_ge(attn_ok, 2 * m.n + 2)
                pe.wait_ge(qst_ok, min(m.n + 3, NB) if isinstance(m.n, int) else m.n + 3)
                for c in range(DK):
                    ins = pe.transpose(M0[:, D + c * P:D + c * P + P], attn[:, c * P:c * P + P], identf[:, :])
                ins.then_inc(attnT_mm, 1)

            def project_out(m):
                pe.wait_ge(attnT_ok, m.n + 1)
                for c in range(DK):
                    ins = pe.matmul(M0[:, 0:D], attnT[:, c, :], WO[:, c, :], start=(c == 0), stop=(c == DK - 1))
                ins.then_inc(wo_mm, 1)

            pe.wait_ge(w_in, 48)

            def period(b):
                m1, m2, m3, o = b + 1, b + 2, b + 3, b + -1
                for g in range(QUADS):
                    if inside(b):
                        logits_k(b, g)
                    if g % 2 == 1:
                        who, half = (b, (g + 3) // 2) if g < 5 else (m1, (g - 5) // 2)
                        if inside(who):
                            transpose_max(who, half)
                    who, u = (b, g + 5) if g < 3 else (m1, g - 3)
                    if inside(who):
                        logits_q(who, u)
                    if g == 0 and inside(m1):
                        project_v(m1)
                    if g == 0 and inside(o):
                        weigh_values(o, QUADS - 1)
                    if g > 0 and inside(b):
                        weigh_values(b, g - 1)
                    if g == 0 and inside(m3):
                        transpose_xc(m3)
                    if g == 1 and inside(m1):
                        transpose_q(m1)
                    if g == 1 and inside(m3):
                        project_k(m3)
                    if g == 2 and inside(m3):
                        project_q(m3)
                    if g == 3 and inside(o):
                        transpose_outputs(o, 1)
                    if g == 4 and inside(o):
                        transpose_attn(o)
                    if g == 5 and inside(m2):
                        transpose_k(m2)
                    if g == 6 and inside(o):
                        project_out(o)
                    if g == 7 and inside(b):
                        transpose_outputs(b, 0)
            periods(pe, period)


def mixture(nc, sem, X, identf, st2, ring, ahead, out):
    G4, R = 4, CAP // 4
    FC = [(0, 128), (128, 128), (256, SHARED - 256)]
    SPLIT = [(c, a, b) for c in range(DK) for a, b in ((0, 0), (0, 1), (1, 0))]
    COUNTED = [r for n in range(R - COUNT_ACT) for r in (n, n + R - COUNT_ACT) if n < COUNT_ACT or r == n]
    AHEAD = 3
    HB = 6
    H_STORED = [16 * len(range(i, NB // 2, HB // 2)) for i in range(HB // 2)]
    ROW = D + NE
    with ExitStack() as es:
        def sb(name, shape, dt=F32):
            return es.enter_context(nc.sbuf_tensor(name, shape, dt))

        table = nc.dram_tensor("table", (T, ROW), F32, kind="Internal").ap()
        gw, WSG, WSD, zero, gw_in, w2_in = ahead.gw, ahead.WSG, ahead.WSD, ahead.zero, ahead.gw_in, ahead.w2_in
        odd = nc.dram_tensor("odd", (T + CAP, D), F32, kind="Internal").ap()
        hT = sb("hT", [P, 2, DK, T], F16)
        mv2 = sb("mv2", [P, NB, 2])
        rs2 = sb("rs2", [P, NB])
        nb2 = sb("nb2", [P, NB])
        gwT = sb("gwT", [P, 2, DK, NE], F16)
        gv = sb("gv", [P, NB, 8])
        gi = sb("gi", [P, NB, 8], U32)
        io8 = sb("io8", [P, GROUPS])
        ex = sb("ex", [P, NB, NE])
        wt = sb("wt", [P, NB, NE])
        smx = sb("smx", [P, NB])
        ssum = sb("ssum", [P, NB])
        eih = sb("eih", [P, NB, 8], F16)
        io32 = sb("io32", [P, NE], F16)
        chosen = sb("chosen", [P, NB, NE], F16)
        tri = sb("tri", [P, 4 * P], F16)
        carry = sb("carry", [P, 4])
        cum = sb("cum", [P, T], F16)
        thr = sb("thr", [P, R])
        thr_half = sb("thr_half", [P, R])
        tok = sb("tok", [P, R])
        toki = sb("toki", [P, R], U32)
        own = sb("own", [P, NE])
        io64 = sb("io64", [P, 2 * LANE])
        place = sb("place", [P, R, 2 * LANE])
        tw = sb("tw", [P, R, 2, NE])
        xg = sb("xg", [P, R, ROW])
        chosen4 = xg[:, :, :].rearrange("p r d -> p (r d)")[:, 0:NB * G4 * NE // 2].bitcast(F16).rearrange("p (b g e) -> p b g e", b=NB, g=G4)
        xbT = sb("xbT", [P, DK, NE * CAP + LANE - CAP])
        sc = xbT[:, 0, 0:NB * NE].rearrange("p (b e) -> p b e", b=NB)
        eq = [xbT[:, 0, (2 + i) * NB * NE // 2:(3 + i) * NB * NE // 2].bitcast(F16).rearrange("p (b e) -> p b e", b=NB) for i in range(3)]
        gm, gif, *kp = (xbT[:, 1, i * NB * 8:(i + 1) * NB * 8].rearrange("p (b g) -> p b g", b=NB) for i in range(2 + TOPG))
        junk, junk2 = (xbT[:, i, 0:T // 2].bitcast(F16) for i in range(2))
        pcol = sb("pcol", [CAP, 1])
        twp = sb("twp", [P, 2, NE])
        wpair = sb("wpair", [P, NPAIR])
        inv = sb("inv", [CAP, NE])
        dst = sb("dst", [CAP, NE], U32)
        sg = [sb(f"sg{i}", [P, 512]) for i in range(2)]
        ac = [sb(f"ac{i}", [P, 3, 512]) for i in range(2)]
        ro = [sb(f"ro{i}", [P, D]) for i in range(2)]
        h = ac[1][:, :, :].rearrange("p f t -> p (f t)").rearrange("p (b d) -> p b d", d=D)
        acf = [ac[i][:, :, :].rearrange("p f t -> p (f t)") for i in range(2)]
        es_ = [acf[i][:, 0:INNER].rearrange("p (m q) -> p m q", m=2) for i in range(2)]
        ea = [acf[i][:, INNER:2 * INNER].rearrange("p (m q) -> p m q", m=2) for i in range(2)]
        eaT = [acf[i][0:IH, 2 * INNER:2 * INNER + 2 * P].rearrange("p (m q) -> p m q", m=2) for i in range(2)]
        ys = [acf[i // 2][:, 640 + D * (i % 2):640 + D * (i % 2) + D] for i in range(3)]
        bank = [es.enter_context(nc.psum_tensor(f"mbank{i}", [P, 512], F32)) for i in range(8)]
        GU, TB, LG = bank[0:4], bank[5:7], bank[7]
        DN = bank[4], bank[7]
        XB = bank[5], bank[0], bank[6], bank[1]
        EB, YB, ET = bank[0:3], bank[3:5], bank[5:7]

        mc_ok, mc2_ok = sem("mc_ok"), sem("mc2_ok")
        mv2_ok, std2, rs2_ok = sem("mv2_ok"), sem("std2"), sem("rs2_ok")
        hT_hi = sem("hT_hi")
        h_ok, h_in, hT_mm, hT_ok = sem("h_ok"), [sem(f"h_in{i}") for i in range(HB // 2)], sem("hT_mm"), sem("hT_ok")
        gwT_mm, gwT_hi, gwT_ok, lgT_mm, lgT_ok, lg_mm = (sem(n) for n in ("gwT_mm", "gwT_hi", "gwT_ok", "lgT_mm", "lgT_ok", "lg_mm"))
        route, sc_ok, ex_ok, wt_ok, wt_in = sem("route"), sem("sc_ok"), sem("ex_ok"), sem("wt_ok"), sem("wt_in")
        chosen_ok, cum_mm, cum_ok = sem("chosen_ok"), sem("cum_mm"), sem("cum_ok")
        cnt_act, cnt_ok, toki_ok, xg_in = sem("cnt_act"), sem("cnt_ok"), sem("toki_ok"), [sem(f"xg_in{r}") for r in range(R)]
        tw_ok, tw_mm, tw48_ok, dst_ok = sem("tw_ok"), sem("tw_mm"), sem("tw48_ok"), sem("dst_ok")
        xb_mm, xb_ok = sem("xb_mm"), [sem("xb_ok_even"), sem("xb_ok_odd")]
        up_mm, sg_ok, ac_ok, dn_mm, ro_ok = sem("up_mm"), sem("sg_ok"), sem("ac_ok"), sem("dn_mm"), sem("ro_ok")
        zero_in = sem("zero_in")
        ac3_ok = sem("ac3_ok")
        dn_ok, ro_in = sem("dn_ok"), sem("ro_in")
        eup_mm, es_ok, ea_ok, eaT_mm, eaT_ok, y_mm, ys_ok = (sem(n) for n in ("eup_mm", "es_ok", "ea_ok", "eaT_mm", "eaT_ok", "y_mm", "ys_ok"))
        sum_in = sem("sum_in")
        add_in = [sem("add_in_even"), sem("add_in_odd")]

        def product(c):
            return (ac_ok, c + 1) if c < 9 else (ac3_ok, c - 8)

        def tiles(k, half=None):
            a = 4 * k + (2 * half if half else 0)
            return range(a, a + (4 if half is None else 2))

        def place_rows(eng, copy, r):
            eng.wait_ge(xb_mm, r + 1)
            for c in range(DK):
                ins = copy(xbT[:, c, 0:NE * CAP].rearrange("p (e g r) -> p r g e", e=NE, g=G4)[:, r],
                           XB[r % 4][:, c * P:c * P + P].rearrange("p (g e) -> p g e", g=G4))
            ins.then_inc(xb_ok[r % 2], 1)

        ring.more(hT[:, :, :, :].rearrange("p a c t -> p (a c t)").bitcast(F32))
        ring.more(X[:, :, :].rearrange("p b d -> p (b d)"))
        block = es.enter_context(nc.Block())

        @block.sync
        def _(sp):
            for j in range(NB // 2):
                sp.wait_ge(h_ok, 2 * j + 2)
                i = j % (HB // 2)
                sp.dma_start(table[2 * j * P:2 * j * P + 2 * P, 0:D].rearrange("(b p) d -> p b d", p=P),
                             h[:, 2 * i:2 * i + 2, :]).then_inc(h_in[i], 16)
            sp.wait_ge(ahead.zero_ok, 1)
            sp.dma_start(out[T:T + CAP, :], zero[0:CAP, :]).then_inc(zero_in, 16)
            sp.dma_start(odd[T:T + CAP, :], zero[0:CAP, :]).then_inc(zero_in, 16)
            sp.dma_start(odd[0:T, :].rearrange("(b p) d -> p b d", p=P), zero[:, :].unsqueeze(1).broadcast_to([P, NB, D])).then_inc(zero_in, 16)
            sp.wait_ge(wt_ok, 1)
            sp.dma_start(table[:, D:ROW].rearrange("(b p) e -> p b e", p=P), wt[:, :, :]).then_inc(wt_in, 16)
            for k in range(4):
                if k == 3:
                    sp.wait_ge(up_mm, 12)
                    ring.load(sp, RESIDENT)
                sp.wait_ge(ro_ok, 4 * k + 4)
                sp.dma_start(out[512 * k:512 * k + 512, :].rearrange("(b p) d -> p b d", p=P), X[:, 4 * k:4 * k + 4, :]).then_inc(ro_in, 16)
            sp.wait_ge(ro_in, 16 * 4)
            ring.load(sp, RESIDENT + 1)
            for k in range(RESIDENT + 2, NPAIR):
                sp.wait_ge(y_mm, k - RESIDENT - 1)
                ring.load(sp, k)

        @block.gpsimd
        def _(pool):
            pool.memset(tri[:, :], 1.0).then_inc(mc_ok, 1)
            pool.memset(carry[:, :], 0.0).then_inc(mc2_ok, 1)
            pool.wait_ge(mc_ok, 1)
            pool.affine_select(out=tri[:, 0:P], in_=tri[:, 0:P], compare_op=ALU.is_ge, fill=0.0, base=0,
                               pattern=[[1, P]], channel_multiplier=-1).then_inc(mc2_ok, 1)
            pool.iota(io8[:, :], [[1, GROUPS]], base=0, channel_multiplier=0, allow_small_or_imprecise_dtypes=True).then_inc(mc2_ok, 1)
            pool.iota(io32[:, :], [[1, NE]], base=0, channel_multiplier=0, allow_small_or_imprecise_dtypes=True).then_inc(mc2_ok, 1)
            pool.iota(io64[:, :], [[0, 2], [1, LANE]], base=0, channel_multiplier=0, allow_small_or_imprecise_dtypes=True).then_inc(mc2_ok, 1)
            pool.memset(xbT[:, :, NE * CAP:], 0.0).then_inc(mc2_ok, 1)
            pool.iota(pcol[:, :], [[0, 1]], base=0, channel_multiplier=1, allow_small_or_imprecise_dtypes=True).then_inc(mc2_ok, 1)
            for g in range(G4):
                rows = slice(NE * g, NE * g + NE)
                pool.wait_ge(mc2_ok, 7 + 2 * g)
                pool.iota(thr[rows, :], [[1, R]], base=R * g, channel_multiplier=0, allow_small_or_imprecise_dtypes=True).then_inc(mc2_ok, 1)
                pool.iota(own[rows, :], [[1, NE]], base=0, channel_multiplier=-1, allow_small_or_imprecise_dtypes=True).then_inc(mc2_ok, 1)

            def gated(k, f):
                n = FC[f][1]
                pool.wait_ge(sg_ok, 3 * k + f + 1)
                pool.tensor_tensor(ac[k % 2][0:n, f, :], ac[k % 2][0:n, f, :], sg[(3 * k + f) % 2][0:n, :], ALU.mult).then_inc(ac_ok, 1)

            def residual(k, half=None):
                for m in tiles(k, half):
                    pool.wait_ge(dn_ok, m + 1)
                    pool.tensor_tensor(X[:, m, :], X[:, m, :], ro[m % 2][:, :], ALU.add).then_inc(ro_ok, 1)

            def gather(i):
                for n in range(3 * i, 3 * i + 3):
                    pool.wait_ge(toki_ok, n + 1)
                    r = COUNTED[n]
                    pool.indirect_dma_start(xg[:, r, :], None, table[:, :], bass.IndirectOffsetOnAxis(ap=toki[:, r:r + 1], axis=0)
                                            ).then_inc(xg_in[r], 16)
            pool.wait_ge(mc2_ok, 7 + 2 * G4)
            for f in range(3):
                gated(0, f)
            gated(1, 0)
            residual(0)
            gated(1, 1)
            gated(1, 2)
            gated(2, 0)
            residual(1)
            for i in range(HB // 2):
                pool.wait_ge(h_in[i], H_STORED[i])
            pool.wait_ge(wt_in, 16)
            gather(0)
            gated(2, 1)
            gather(1)
            gated(2, 2)
            gather(2)
            gather(3)
            residual(2)
            residual(3)
            pool.wait_ge(zero_in, 48)
            pool.wait_ge(ro_in, 16 * 4)

            for k in range(NPAIR):
                for w, to in ((0, out), (1, odd)):
                    rows = slice(LANE * w, LANE * w + CAP)
                    pool.wait_ge(ys_ok, k + 1)
                    at_least(pool, add_in[w], 16 * k)
                    pool.indirect_dma_start(to[:, :], bass.IndirectOffsetOnAxis(ap=dst[:, 2 * k + w:2 * k + w + 1], axis=0),
                                            ys[k % 3][rows, :], None, compute_op=ALU.add).then_inc(add_in[w], 16)
            for w in range(2):
                pool.wait_ge(add_in[w], 16 * NPAIR)
            pool.dma_start(out[0:T, :], odd[0:T, :], accum_op=ALU.add, max_dma_last_dim=8192).then_inc(sum_in, 16)
            pool.wait_ge(sum_in, 16)

        @block.scalar
        def _(act):
            act.wait_ge(mv2_ok, 2)
            act.activation(rs2[:, :], nb2[:, :], ACT.Sqrt).then_inc(std2, 1)
            act.wait_ge(gwT_mm, 1)
            act.activation(gwT[:, 0], TB[0][:, 0:DK * NE].rearrange("p (c e) -> p c e", c=DK), ACT.Copy, scale=WUP).then_inc(gwT_hi, 1)
            act.wait_ge(rs2_ok, 2)

            def norm(m):
                at_least(act, hT_mm, m - HB + 1)
                at_least(act, h_in[m % HB // 2], 16 * (m // HB))
                act.activation(h[:, m % HB, :], X[:, m, :], ACT.Identity, bias=nb2[:, m:m + 1],
                               scale=rs2[:, m:m + 1]).then_inc(h_ok, 1)

            def hi(m):
                act.wait_ge(hT_mm, m + 1)
                act.copy(hT[:, 0, :, m * P:m * P + P], TB[m % 2][:, 0:D].rearrange("p (c t) -> p c t", c=DK)).then_inc(hT_hi, 1)
            for m in range(NB + AHEAD):
                if m < NB:
                    norm(m)
                if m >= AHEAD:
                    hi(m - AHEAD)

            def gate(k, f):
                c, n = 3 * k + f, FC[f][1]
                act.wait_ge(up_mm, c + 1)
                if c > 1:
                    act.wait_ge(*product(c - 2))
                act.activation(sg[c % 2][0:n, :], GU[2 * (c % 2)][0:n, :], ACT.Silu, scale=1 / WUP)
                if c == 3:
                    for i in range(HB // 2):
                        act.wait_ge(h_in[i], H_STORED[i])
                at_least(act, dn_mm, 4 * (k - 1))
                act.activation(ac[k % 2][0:n, f, :], GU[2 * (c % 2) + 1][0:n, :], ACT.Copy, scale=1 / WUP).then_inc(sg_ok, 1)

            def shared_rows(k, half=None):
                for m in tiles(k, half):
                    act.wait_ge(dn_mm, m + 1)
                    at_least(act, ro_ok, m - 1)
                    act.copy(ro[m % 2][:, :], DN[m % 2][:, 0:D]).then_inc(dn_ok, 1)

            def count(n):
                r = R - COUNT_ACT + n
                if n == 0:
                    act.wait_ge(cum_ok, 4)
                    act.wait_ge(cnt_ok, 1)
                else:
                    act.wait_ge(cnt_act, n)
                act.activation(junk2, cum[:, :], ACT.Sign, bias=thr_half[:, r:r + 1], scale=-1.0,
                               accum_out=tok[:, r:r + 1]).then_inc(cnt_act, 1)
            act.wait_ge(lg_mm, 4)
            gate(0, 0)
            gate(0, 1)
            act.wait_ge(sc_ok, 1)
            act.activation(ex[:, :, :], sc[:, :, :], ACT.Exp).then_inc(ex_ok, 1)
            gate(0, 2)
            gate(1, 0)
            shared_rows(0)
            gate(1, 1)
            gate(1, 2)
            count(0)
            gate(2, 0)
            count(1)
            shared_rows(1)
            count(2)
            gate(2, 1)
            count(3)
            gate(2, 2)
            gate(3, 0)
            gate(3, 1)
            shared_rows(2, 0)
            gate(3, 2)
            shared_rows(2, 1)
            shared_rows(3)
            act.wait_ge(toki_ok, R)
            for r in range(0, R, 2):
                place_rows(act, act.copy, r)

            def evac_eaT(k):
                act.wait_ge(eaT_mm, k + 1)
                at_least(act, y_mm, k - 1)
                act.copy(eaT[k % 2][:, :, :], ET[k % 2][0:IH, 0:2 * P].rearrange("p (m q) -> p m q", m=2)).then_inc(eaT_ok, 1)
            for k in range(NPAIR):
                act.wait_ge(eup_mm, k + 1)
                at_least(act, ea_ok, k - 1)
                act.activation(es_[k % 2][:, :, :], EB[k % 3][:, 0:INNER].rearrange("p (q m) -> p m q", m=2), ACT.Silu).then_inc(es_ok, 1)
                if k == 0:
                    evac_eaT(0)
                if k > 1:
                    evac_eaT(k - 1)
            evac_eaT(NPAIR - 1)

        @block.vector
        def _(dve):
            done = [0]

            def step(ins):
                done[0] += 1
                ins.then_inc(route, 1)
                dve.wait_ge(route, done[0])

            for m in range(NB):
                ins = dve.bn_aggr(mv2[:, m, :], st2[:, m, :])
            ins.then_inc(mv2_ok, 1)
            dve.wait_ge(mv2_ok, 1)
            dve.tensor_scalar(nb2[:, :], mv2[:, :, 1], EPS, None, ALU.add).then_inc(mv2_ok, 1)
            dve.wait_ge(std2, 1)
            dve.reciprocal(rs2[:, :], rs2[:, :]).then_inc(rs2_ok, 1)
            dve.wait_ge(rs2_ok, 1)
            dve.scalar_tensor_tensor(out=nb2[:, :], in0=mv2[:, :, 0], scalar=-1.0, in1=rs2[:, :],
                                     op0=ALU.mult, op1=ALU.mult).then_inc(rs2_ok, 1)

            dve.wait_ge(gwT_hi, 1)
            dve.scalar_tensor_tensor(out=gwT[:, 1], in0=TB[0][:, 0:DK * NE].rearrange("p (c e) -> p c e", c=DK), scalar=WUP,
                                     in1=gwT[:, 0], op0=ALU.mult, op1=ALU.subtract).then_inc(gwT_ok, 1)

            def evac_logits(k):
                dve.wait_ge(lgT_mm, k + 1)
                at_least(dve, lg_mm, k - 1)
                dve.tensor_scalar(sg[k % 2][0:NE, :], DN[0][0:NE, :], 1 / WUP, None, ALU.mult).then_inc(lgT_ok, 1)
            for m in range(NB):
                rows, part = TB[m % 2][:, 0:D].rearrange("p (c t) -> p c t", c=DK), slice(m * P, m * P + P)
                dve.wait_ge(hT_hi, m + 1)
                dve.tensor_tensor(hT[:, 1, :, part], rows, hT[:, 0, :, part], ALU.subtract).then_inc(hT_ok, 1)
                if m % 4 == 1 and m > 4:
                    evac_logits(m // 4 - 1)
            evac_logits(3)

            dve.wait_ge(lg_mm, 4)
            dve.wait_ge(mc2_ok, 7 + 2 * G4)
            lg = LG[:, :].rearrange("p (b g k) -> p b g k", b=NB, g=GROUPS)
            step(dve.tensor_reduce(gm[:, :, :], lg, axis=AX.X, op=ALU.max))
            for m in range(NB):
                ins = dve.max(gv[:, m, :], gm[:, m, :])
            step(ins)
            for m in range(NB):
                ins = dve.max_index(gi[:, m, :], gv[:, m, :], gm[:, m, :])
            step(ins)
            step(dve.tensor_copy(gif[:, :, :], gi[:, :, :]))
            for k in range(TOPG):
                ins = dve.tensor_tensor(kp[k][:, :, :], io8[:, :].unsqueeze(1).broadcast_to([P, NB, GROUPS]),
                                        gif[:, :, k].unsqueeze(2).broadcast_to([P, NB, GROUPS]), ALU.is_equal)
            step(ins)
            step(dve.tensor_tensor(kp[0][:, :, :], kp[0][:, :, :], kp[1][:, :, :], ALU.add))
            step(dve.tensor_tensor(kp[0][:, :, :], kp[0][:, :, :], kp[2][:, :, :], ALU.add))
            step(dve.tensor_tensor(sc[:, :, :].rearrange("p b (g k) -> p b g k", g=GROUPS), lg,
                                   kp[0][:, :, :].unsqueeze(3).broadcast_to([P, NB, GROUPS, NE // GROUPS]), ALU.mult))
            step(dve.tensor_reduce(smx[:, :], sc[:, :, :], axis=AX.X, op=ALU.max))
            dve.tensor_tensor(sc[:, :, :], sc[:, :, :], smx[:, :].unsqueeze(2).broadcast_to([P, NB, NE]), ALU.subtract).then_inc(sc_ok, 1)
            dve.wait_ge(ex_ok, 1)
            step(dve.tensor_reduce(ssum[:, :], ex[:, :, :], axis=AX.X, op=ALU.add))
            step(dve.reciprocal(smx[:, :], ssum[:, :]))
            dve.scalar_tensor_tensor(out=wt[:, :, :], in0=ex[:, :, :], scalar=ROUTE_SCALE,
                                     in1=smx[:, :].unsqueeze(2).broadcast_to([P, NB, NE]), op0=ALU.mult, op1=ALU.mult).then_inc(wt_ok, 1)
            for m in range(NB):
                ins = dve.max(gv[:, m, :], ex[:, m, :])
            step(ins)
            for m in range(NB):
                ins = dve.max_index(gi[:, m, :], gv[:, m, :], ex[:, m, :])
            step(ins)
            step(dve.tensor_copy(eih[:, :, :], gi[:, :, :]))

            def mask(k):
                to = chosen if k == 0 else eq[k % 3]
                done[0] += 1
                dve.tensor_tensor(to[:, :, :], io32[:, :].unsqueeze(1).broadcast_to([P, NB, NE]),
                                  eih[:, :, k].unsqueeze(2).broadcast_to([P, NB, NE]), ALU.is_equal).then_inc(route, 1)
            mask(0)
            mask(1)
            for k in range(1, TOPK):
                made = done[0]
                if k + 1 < TOPK:
                    mask(k + 1)
                dve.wait_ge(route, made)
                done[0] += 1
                dve.tensor_tensor(chosen[:, :, :], chosen[:, :, :], eq[k % 3][:, :, :], ALU.add).then_inc(route, 1)
            dve.wait_ge(route, done[0])
            for g in range(G4):
                ins = dve.tensor_copy(chosen4[:, :, g, :], chosen[:, :, :])
            ins.then_inc(chosen_ok, 1)
            step(dve.tensor_scalar(own[:, :], own[:, :], 0.0, None, ALU.is_equal))
            step(dve.tensor_tensor(place[:, :, :], io64[:, :].unsqueeze(1).broadcast_to([P, R, 2 * LANE]),
                                   thr[:, :].unsqueeze(2).broadcast_to([P, R, 2 * LANE]), ALU.is_equal))
            dve.tensor_scalar(thr_half[:, :], thr[:, :], 0.5, None, ALU.add).then_inc(cnt_ok, 1)
            for c in range(4):
                dve.wait_ge(cum_mm, c + 1)
                if c < 3:
                    step(dve.tensor_tensor(carry[:, c + 1:c + 2], carry[:, c:c + 1], TB[c % 2][:, 511:512], ALU.add))
                dve.tensor_scalar(cum[:, 512 * c:512 * c + 512], TB[c % 2][:, :], carry[:, c:c + 1], None, ALU.add).then_inc(cum_ok, 1)
            dve.wait_ge(cum_ok, 4)

            for n, r in enumerate(COUNTED):
                if r < R - COUNT_ACT:
                    step(dve.tensor_scalar(junk, cum[:, :], thr[:, r:r + 1], None, ALU.is_le, ALU.add,
                                           accum_out=tok[:, r:r + 1]))
                else:
                    dve.wait_ge(cnt_act, r - (R - COUNT_ACT) + 1)
                    step(dve.tensor_scalar(tok[:, r:r + 1], tok[:, r:r + 1], 0.5, T / 2, ALU.mult, ALU.add))
                dve.tensor_scalar(toki[:, r:r + 1], tok[:, r:r + 1], float(T - 1), None, ALU.min).then_inc(toki_ok, 1)
            for f in range(3):
                n = FC[f][1]
                dve.wait_ge(sg_ok, 9 + f + 1)
                dve.tensor_tensor(ac[1][0:n, f, :], ac[1][0:n, f, :], sg[(9 + f) % 2][0:n, :], ALU.mult).then_inc(ac3_ok, 1)
            own_r = own[:, :].unsqueeze(1).broadcast_to([P, R, NE])
            dve.tensor_tensor(tw[:, :, 0, :], own_r, tok[:, :].unsqueeze(2).broadcast_to([P, R, NE]), ALU.mult)
            for r in range(1, R, 2):
                place_rows(dve, dve.tensor_copy, r)
            for r in range(R):
                dve.wait_ge(xg_in[r], 16)
            dve.tensor_tensor(tw[:, :, 1, :], own_r, xg[:, :, D:ROW], ALU.mult).then_inc(tw_ok, 1)

            def places():
                dve.wait_ge(tw_mm, 1)
                step(dve.tensor_copy(twp[:, :, :], LG[:, 0:2 * NE].rearrange("p (a e) -> p a e", a=2)))
                step(dve.tensor_scalar(inv[:, :], twp[0:CAP, 0, :], float(T), pcol[:, :], ALU.is_ge, ALU.mult))
                dve.tensor_tensor(dst[:, :], inv[:, :], twp[0:CAP, 0, :], ALU.add)
                for w in range(2):
                    rows = slice(LANE * w, LANE * w + LANE)
                    step(dve.tensor_copy(wpair[rows, :], twp[rows, 1, w:NE:2]))

            def weighted(k):
                dve.wait_ge(y_mm, k + 1)
                for w in range(2):
                    at_least(dve, add_in[w], 16 * (k - 2))
                dve.tensor_scalar(ys[k % 3][:, :], YB[k % 2][:, 0:D], wpair[:, k:k + 1], None, ALU.mult).then_inc(ys_ok, 1)
            for k in range(NPAIR):
                dve.wait_ge(es_ok, k + 1)
                at_least(dve, eaT_mm, k - 1)
                dve.tensor_tensor(ea[k % 2][:, :, :], EB[k % 3][:, INNER:2 * INNER].rearrange("p (q m) -> p m q", m=2),
                                  es_[k % 2][:, :, :], ALU.mult).then_inc(ea_ok, 1)
                if k == 0:
                    places()
                    weighted(0)
                if k > 2:
                    weighted(k - 2)
            weighted(NPAIR - 2)
            weighted(NPAIR - 1)

        @block.tensor
        def _(pe):
            pe.wait_ge(gw_in, 16)
            for c in range(DK):
                ins = pe.transpose(TB[0][:, c * NE:c * NE + NE], gw[:, c * P:c * P + P], identf[0:NE, 0:NE])
            ins.then_inc(gwT_mm, 1)
            pe.wait_ge(gwT_ok, 1)

            def logits(k):
                pe.wait_ge(hT_ok, 4 * k + 4)
                at_least(pe, lgT_ok, k)
                for i, (c, a, b) in enumerate(SPLIT):
                    ins = pe.matmul(DN[0][0:NE, :], gwT[:, a, c, :], hT[:, b, c, 512 * k:512 * k + 512],
                                    start=(i == 0), stop=(i == len(SPLIT) - 1))
                ins.then_inc(lgT_mm, 1)

            def turn_logits(k):
                pe.wait_ge(lgT_ok, k + 1)
                for m in range(4 * k, 4 * k + 4):
                    ins = pe.transpose(LG[:, m * NE:m * NE + NE], sg[k % 2][0:NE, (m - 4 * k) * P:(m - 4 * k) * P + P], identf[0:NE, 0:NE])
                ins.then_inc(lg_mm, 1)
            for m in range(NB):
                pe.wait_ge(h_ok, m + 1)
                at_least(pe, hT_ok, m - 1)
                for c in range(DK):
                    ins = pe.transpose(TB[m % 2][:, c * P:c * P + P], h[:, m % HB, c * P:c * P + P], identf[:, :])
                ins.then_inc(hT_mm, 1)
                if m % 4 == 1 and m > 4:
                    logits(m // 4 - 1)
                if m % 4 == 3 and m > 4:
                    turn_logits(m // 4 - 1)
            logits(3)
            turn_logits(3)
            pe.wait_ge(ahead.wsg_lo, 1)
            pe.wait_ge(w2_in, 16 * 2)

            def up(k, f):
                i, (a, n) = 3 * k + f, FC[f]
                at_least(pe, sg_ok, i - 1)
                for w in range(2):
                    for j, (c, u, v) in enumerate(SPLIT):
                        ins = pe.matmul(GU[2 * (i % 2) + w][0:n, :], WSG[:, c, u, w * SHARED + a:w * SHARED + a + n],
                                        hT[:, v, c, 512 * k:512 * k + 512], start=(j == 0), stop=(j == len(SPLIT) - 1))
                ins.then_inc(up_mm, 1)

            def down(m):
                k, j = m // 4, m % 4
                pe.wait_ge(*product(3 * k + 2))
                at_least(pe, dn_ok, m - 1)
                if m == 1:
                    pe.wait_ge(sc_ok, 1)
                for f in range(3):
                    n = FC[f][1]
                    ins = pe.matmul(DN[m % 2][:, 0:D], ac[k % 2][0:n, f, j * P:j * P + P], WSD[0:n, f, :], start=(f == 0), stop=(f == 2))
                ins.then_inc(dn_mm, 1)

            def cumulate(c):
                at_least(pe, cum_ok, c - 1)
                for i in range(4):
                    ins = pe.matmul(TB[c % 2][:, i * P:512], chosen4[:, 4 * c + i, :, :], tri[:, 0:512 - i * P], start=(i == 0), stop=(i == 3))
                ins.then_inc(cum_mm, 1)

            for f in range(3):
                up(0, f)
            up(1, 0)
            for m in range(4):
                down(m)
            up(1, 1)
            up(1, 2)
            pe.wait_ge(chosen_ok, 1)
            for c in range(4):
                cumulate(c)
            up(2, 0)
            for m in range(4, 8):
                down(m)
            up(2, 1)
            up(2, 2)
            up(3, 0)
            up(3, 1)
            for m in tiles(2, 0):
                down(m)
            up(3, 2)
            for m in (*tiles(2, 1), *tiles(3)):
                down(m)
            pe.wait_ge(sg_ok, 12)
            for r in range(R):
                pe.wait_ge(xg_in[r], 16)
                at_least(pe, xb_ok[r % 2], r // 2 - 1)
                for c in range(DK):
                    ins = pe.transpose(XB[r % 4][:, c * P:c * P + P], xg[:, r, c * P:c * P + P], identf[:, :])
                ins.then_inc(xb_mm, 1)

            def tokens_weights():
                pe.wait_ge(tw_ok, 1)
                pe.wait_ge(dn_ok, NB)
                for r in range(R):
                    ins = pe.matmul(LG[:, 0:2 * NE], place[:, r, :], tw[:, r, :, :], start=(r == 0), stop=(r == R - 1))
                ins.then_inc(tw_mm, 1)
            for w in range(2):
                pe.wait_ge(xb_ok[w], R // 2)

            def pair_up(k):
                place = k % len(ring.gu)
                ring.wait(pe, k)
                for c in range(DK):
                    for e in (2 * k, 2 * k + 1):
                        lane = slice(LANE * (e % 2), LANE * (e % 2) + LANE)
                        ins = pe.matmul(EB[k % 3][lane, 0:2 * INNER], xbT[:, c, e * CAP:e * CAP + LANE], ring.gu[place][:, e % 2, c, :],
                                        start=(c == 0), stop=(c == DK - 1), tile_position=(0, LANE * (e % 2)))
                ins.then_inc(eup_mm, 1)

            def pair_turn(k):
                pe.wait_ge(ea_ok, k + 1)
                at_least(pe, eaT_ok, k - 1)
                for m in range(2):
                    ins = pe.transpose(ET[k % 2][0:IH, m * P:m * P + P], ea[k % 2][:, m, :], identf[:, :])
                ins.then_inc(eaT_mm, 1)

            def pair_down(k):
                place = k % len(ring.gu)
                pe.wait_ge(eaT_ok, k + 1)
                at_least(pe, ys_ok, k - 1)
                for m in range(2):
                    for e in (2 * k, 2 * k + 1):
                        lane = slice(LANE * (e % 2), LANE * (e % 2) + LANE)
                        ins = pe.matmul(YB[k % 2][lane, 0:D], eaT[k % 2][:, m, lane], ring.dn[place][:, e % 2, m, :],
                                        start=(m == 0), stop=(m == 1), tile_position=(0, LANE * (e % 2)))
                ins.then_inc(y_mm, 1)
            for k in range(NPAIR):
                at_least(pe, ea_ok, k - 2)
                pair_up(k)
                if k == 0:
                    tokens_weights()
                    pair_turn(0)
                    pair_down(0)
                if k > 1:
                    pair_turn(k - 1)
                if k > 2:
                    pair_down(k - 2)
            pair_turn(NPAIR - 1)
            pair_down(NPAIR - 2)
            pair_down(NPAIR - 1)


_INS = ["x", "ctx_1024", "fside_BxSx2_0", "L0_xattn_Wq", "L0_xattn_Wkv", "L0_xattn_Wout", "L0_xattn_bout",
        "L0_ffn_gate_w", "L0_ffn_w_gate_up", "L0_ffn_w_down", "L0_ffn_ws_gate_up", "L0_ffn_ws_down"]


def kernel(**inputs):
    import concourse.bacc as bacc
    from concourse.bass_utils import run_bass_kernel_spmd

    nc = bacc.Bacc("TRN2", target_bir_lowering=False, num_devices=1)
    arrays, args = {}, []
    for name in _INS:
        a = np.ascontiguousarray(inputs[name])
        arrays[f"in_{name}"] = a
        args.append(nc.dram_tensor(f"in_{name}", a.shape, F32, kind="ExternalInput").ap())
    out = nc.dram_tensor("out", (T + CAP, D), F32, kind="ExternalOutput").ap()
    build(nc, *args, out)
    r = run_bass_kernel_spmd(nc, [arrays], core_ids=[0])
    return r.results[0]["out"][:T].reshape(NB, P, D)
```
